# Optimizing a Trainium2 kernel written in Bass

```python
import numpy as np
import jax
import jax.numpy as jnp

def _softmax(x, axis=-1):
    return jax.nn.softmax(x, axis=axis)

def _gelu(x):
    return jax.nn.gelu(x, approximate=True)

def _silu(x):
    return jax.nn.silu(x)

def _sigmoid(x):
    return jax.nn.sigmoid(x)

def _layernorm(x, axis=-1, eps=1e-05):
    m = jnp.mean(x, axis=axis, keepdims=True)
    v = jnp.var(x, axis=axis, keepdims=True)
    return (x - m) / jnp.sqrt(v + eps)

def _scatter_add(tgt, idx, src, axis=0):
    return tgt.at[idx].add(src)

def _segment_sum(src, seg, n):
    return jax.ops.segment_sum(src, seg, n)
kernel_name = 'mk_adj_ffn_d1_adj_r2_3f86c5'

def setup_inputs(seed: int=0):
    np.random.seed(seed)
    _w = jnp.asarray

    def _rec_inputs():
        import jax
        import jax.numpy as jnp
        _gk = jax.random.key(seed)
        x = 7.22e-05 + 1 * jax.random.normal(jax.random.fold_in(_gk, 1), (8, 2048, 128), jnp.float32)
        _a = jax.random.bernoulli(jax.random.fold_in(_gk, 2), 0.000976562, (2048, 2048))
        _a = jnp.logical_or(_a, jnp.swapaxes(_a, -1, -2))
        _a = jnp.logical_or(_a, jnp.eye(2048, dtype=bool))
        _af = _a.astype(jnp.float32)
        _af = _af * jax.random.uniform(jax.random.fold_in(_gk, 3), (2048, 2048), jnp.float32, 0.05, 0.119748)
        adj = _af
        return (x, adj)
    x, adj = _rec_inputs()

    def _L0_gnn_setup():
        import jax, jax.numpy as jnp
        import numpy as np
        B, N, F_IN, F_OUT = (8, 2048, 128, 128)
        key = jax.random.key(seed)
        k1, k2, k3 = jax.random.split(key, 3)
        H = jax.random.normal(k1, (B, N, F_IN), dtype=jnp.float32)
        W = jax.random.normal(k2, (F_IN, F_OUT), dtype=jnp.float32) * (1.0 / np.sqrt(F_IN))
        A = jax.random.normal(k3, (N, N), dtype=jnp.float32) * (1.414 * np.sqrt(2.0 / (N + N)))
        return {'H': H, 'W': W, 'A': A}
    _L0_gnn_all = _L0_gnn_setup()
    _L0_gnn_in = {k: v for k, v in _L0_gnn_all.items() if k in ('W',)}
    del _L0_gnn_all

    def _L0_ffn_setup():
        import jax, jax.numpy as jnp
        import numpy as np
        D_MODEL = 128
        D_STATE = 64
        D_CONV = 4
        EXPAND = 2
        HEADDIM = 64
        D_INNER = EXPAND * D_MODEL
        NHEADS = D_INNER // HEADDIM
        CONV_DIM = D_INNER + 2 * D_STATE
        D_IN_PROJ = 2 * D_INNER + 2 * D_STATE + NHEADS
        CHUNK = 128
        EPS = 1e-05

        def segsum(a):
            T = a.shape[-1]
            cs = jnp.cumsum(a, axis=-1)
            ss = cs[..., :, None] - cs[..., None, :]
            mask = jnp.tril(jnp.ones((T, T), dtype=bool))
            return jnp.where(mask, ss, -jnp.inf)

        def mamba2_block(x, W_in, conv_w, conv_b, dt_bias, A_log, D, norm_w, W_out, W_lin, b_lin):
            Bsz, L, _ = x.shape
            zxbcdt = x @ W_in
            z, xBC, dt = jnp.split(zxbcdt, [D_INNER, D_INNER + CONV_DIM], axis=-1)
            xp = jnp.pad(xBC, ((0, 0), (D_CONV - 1, 0), (0, 0)))
            conv = conv_b + sum((xp[:, k:k + L, :] * conv_w[:, k] for k in range(D_CONV)))
            xBC = jax.nn.silu(conv)
            xh, Bmat, Cmat = jnp.split(xBC, [D_INNER, D_INNER + D_STATE], axis=-1)
            dt = jax.nn.softplus(dt + dt_bias)
            A = -jnp.exp(A_log)
            nc = L // CHUNK
            xh = xh.reshape(Bsz, nc, CHUNK, NHEADS, HEADDIM)
            Bc = Bmat.reshape(Bsz, nc, CHUNK, D_STATE)
            Cc = Cmat.reshape(Bsz, nc, CHUNK, D_STATE)
            dtc = dt.reshape(Bsz, nc, CHUNK, NHEADS)
            dA = jnp.einsum('bclh,h->bhcl', dtc, A)
            A_cum = jnp.cumsum(dA, axis=-1)
            Lmat = jnp.exp(segsum(dA))
            xdt = xh * dtc[..., None]
            Y_diag = jnp.einsum('bcln,bcsn,bhcls,bcshp->bclhp', Cc, Bc, Lmat, xdt)
            decay_states = jnp.exp(A_cum[..., -1:] - A_cum)
            states = jnp.einsum('bcln,bhcl,bclhp->bchpn', Bc, decay_states, xdt)
            chunk_decay = jnp.exp(A_cum[..., -1])

            def step(h, inp):
                s, d = inp
                return (h * d[..., None, None] + s, h)
            _, prevs = jax.lax.scan(step, jnp.zeros_like(states[:, 0]), (jnp.moveaxis(states, 1, 0), jnp.moveaxis(chunk_decay, 2, 0)))
            prevs = jnp.moveaxis(prevs, 0, 1)
            Y_off = jnp.einsum('bcln,bchpn,bhcl->bclhp', Cc, prevs, jnp.exp(A_cum))
            Y = (Y_diag + Y_off + xh * D[:, None]).reshape(Bsz, L, D_INNER)
            Y = Y * jax.nn.silu(z)
            Y = Y * jax.lax.rsqrt(jnp.mean(Y * Y, axis=-1, keepdims=True) + EPS) * norm_w
            out = Y @ W_out
            return out @ W_lin + b_lin
        key = jax.random.key(seed)
        ks = jax.random.split(key, 12)
        B, L = (8, 2048)

        def gauss(k, shape, scale):
            return jax.random.normal(k, shape, dtype=jnp.float32) * scale
        return {'x': gauss(ks[0], (B, L, D_MODEL), 1.0), 'W_in': gauss(ks[1], (D_MODEL, D_IN_PROJ), D_MODEL ** (-0.5)), 'conv_w': gauss(ks[2], (CONV_DIM, D_CONV), 0.3), 'conv_b': gauss(ks[3], (CONV_DIM,), 0.1), 'dt_bias': jax.random.uniform(ks[4], (NHEADS,), minval=-4.0, maxval=-1.0), 'A_log': jnp.log(jax.random.uniform(ks[5], (NHEADS,), minval=1.0, maxval=16.0)), 'D': jnp.ones((NHEADS,), jnp.float32), 'norm_w': jnp.ones((D_INNER,), jnp.float32), 'W_out': gauss(ks[6], (D_INNER, D_MODEL), D_INNER ** (-0.5)), 'W_lin': gauss(ks[7], (D_MODEL, D_MODEL), D_MODEL ** (-0.5)), 'b_lin': jnp.zeros((D_MODEL,), jnp.float32)}
    _L0_ffn_all = _L0_ffn_setup()
    _L0_ffn_in = {k: v for k, v in _L0_ffn_all.items() if k in ('W_in', 'conv_w', 'conv_b', 'dt_bias', 'A_log', 'D', 'norm_w', 'W_out', 'W_lin', 'b_lin')}
    del _L0_ffn_all
    return {'x': x, 'adj': adj, 'L0_gnn_W': _L0_gnn_in['W'], 'L0_ffn_W_in': _L0_ffn_in['W_in'], 'L0_ffn_conv_w': _L0_ffn_in['conv_w'], 'L0_ffn_conv_b': _L0_ffn_in['conv_b'], 'L0_ffn_dt_bias': _L0_ffn_in['dt_bias'], 'L0_ffn_A_log': _L0_ffn_in['A_log'], 'L0_ffn_D': _L0_ffn_in['D'], 'L0_ffn_norm_w': _L0_ffn_in['norm_w'], 'L0_ffn_W_out': _L0_ffn_in['W_out'], 'L0_ffn_W_lin': _L0_ffn_in['W_lin'], 'L0_ffn_b_lin': _L0_ffn_in['b_lin']}

def reference(x, adj, L0_gnn_W, L0_ffn_W_in, L0_ffn_conv_w, L0_ffn_conv_b, L0_ffn_dt_bias, L0_ffn_A_log, L0_ffn_D, L0_ffn_norm_w, L0_ffn_W_out, L0_ffn_W_lin, L0_ffn_b_lin):
    import jax
    import jax.numpy as jnp

    def _L0_gnn_ref(H, W, A):
        import jax, jax.numpy as jnp
        import numpy as np
        B, N, F_IN, F_OUT = (8, 2048, 128, 128)
        HW = jnp.einsum('bnf,fo->bno', H, W)
        A_norm = jax.nn.relu((A + A.T) * 0.5)
        D = jnp.sum(A_norm, axis=1)
        D_safe = jnp.where(D > 0, D, 1.0)
        d_inv_sqrt = jnp.where(D > 0, D_safe ** (-0.5), 0.0)
        DAD = d_inv_sqrt[:, None] * A_norm * d_inv_sqrt[None, :]
        L_norm = jnp.eye(N, dtype=H.dtype) - DAD
        out = jnp.einsum('nm,bmo->bno', L_norm, HW)
        return jax.nn.relu(out)

    def _L0_ffn_ref(x, W_in, conv_w, conv_b, dt_bias, A_log, D, norm_w, W_out, W_lin, b_lin):
        import jax, jax.numpy as jnp
        import numpy as np
        D_MODEL = 128
        D_STATE = 64
        D_CONV = 4
        EXPAND = 2
        HEADDIM = 64
        D_INNER = EXPAND * D_MODEL
        NHEADS = D_INNER // HEADDIM
        CONV_DIM = D_INNER + 2 * D_STATE
        D_IN_PROJ = 2 * D_INNER + 2 * D_STATE + NHEADS
        CHUNK = 128
        EPS = 1e-05

        def segsum(a):
            T = a.shape[-1]
            cs = jnp.cumsum(a, axis=-1)
            ss = cs[..., :, None] - cs[..., None, :]
            mask = jnp.tril(jnp.ones((T, T), dtype=bool))
            return jnp.where(mask, ss, -jnp.inf)

        def mamba2_block(x, W_in, conv_w, conv_b, dt_bias, A_log, D, norm_w, W_out, W_lin, b_lin):
            Bsz, L, _ = x.shape
            zxbcdt = x @ W_in
            z, xBC, dt = jnp.split(zxbcdt, [D_INNER, D_INNER + CONV_DIM], axis=-1)
            xp = jnp.pad(xBC, ((0, 0), (D_CONV - 1, 0), (0, 0)))
            conv = conv_b + sum((xp[:, k:k + L, :] * conv_w[:, k] for k in range(D_CONV)))
            xBC = jax.nn.silu(conv)
            xh, Bmat, Cmat = jnp.split(xBC, [D_INNER, D_INNER + D_STATE], axis=-1)
            dt = jax.nn.softplus(dt + dt_bias)
            A = -jnp.exp(A_log)
            nc = L // CHUNK
            xh = xh.reshape(Bsz, nc, CHUNK, NHEADS, HEADDIM)
            Bc = Bmat.reshape(Bsz, nc, CHUNK, D_STATE)
            Cc = Cmat.reshape(Bsz, nc, CHUNK, D_STATE)
            dtc = dt.reshape(Bsz, nc, CHUNK, NHEADS)
            dA = jnp.einsum('bclh,h->bhcl', dtc, A)
            A_cum = jnp.cumsum(dA, axis=-1)
            Lmat = jnp.exp(segsum(dA))
            xdt = xh * dtc[..., None]
            Y_diag = jnp.einsum('bcln,bcsn,bhcls,bcshp->bclhp', Cc, Bc, Lmat, xdt)
            decay_states = jnp.exp(A_cum[..., -1:] - A_cum)
            states = jnp.einsum('bcln,bhcl,bclhp->bchpn', Bc, decay_states, xdt)
            chunk_decay = jnp.exp(A_cum[..., -1])

            def step(h, inp):
                s, d = inp
                return (h * d[..., None, None] + s, h)
            _, prevs = jax.lax.scan(step, jnp.zeros_like(states[:, 0]), (jnp.moveaxis(states, 1, 0), jnp.moveaxis(chunk_decay, 2, 0)))
            prevs = jnp.moveaxis(prevs, 0, 1)
            Y_off = jnp.einsum('bcln,bchpn,bhcl->bclhp', Cc, prevs, jnp.exp(A_cum))
            Y = (Y_diag + Y_off + xh * D[:, None]).reshape(Bsz, L, D_INNER)
            Y = Y * jax.nn.silu(z)
            Y = Y * jax.lax.rsqrt(jnp.mean(Y * Y, axis=-1, keepdims=True) + EPS) * norm_w
            out = Y @ W_out
            return out @ W_lin + b_lin
        return mamba2_block(x, W_in, conv_w, conv_b, dt_bias, A_log, D, norm_w, W_out, W_lin, b_lin)
    x = x + _L0_gnn_ref(_layernorm(x, axis=-1), L0_gnn_W, adj)
    x = x + _L0_ffn_ref(_layernorm(x, axis=-1), L0_ffn_W_in, L0_ffn_conv_w, L0_ffn_conv_b, L0_ffn_dt_bias, L0_ffn_A_log, L0_ffn_D, L0_ffn_norm_w, L0_ffn_W_out, L0_ffn_W_lin, L0_ffn_b_lin)
    return x

_drawn_inputs = setup_inputs


def setup_inputs(seed=0):
    import zlib

    import numpy as np

    out = dict(_drawn_inputs(seed))
    spreads = {'L0_ffn_D': (1.0, 0.2), 'L0_ffn_norm_w': (1.0, 0.2), 'L0_ffn_b_lin': (0.0, 0.1)}
    factors = {'L0_ffn_A_log': 6.382}
    for name, (base, spread) in spreads.items():
        noise = np.random.default_rng([zlib.crc32(name.encode()), seed]).standard_normal(out[name].shape)
        drawn = base * np.exp(spread * noise) if base else spread * noise
        out[name] = jnp.asarray(drawn.astype(out[name].dtype))
    for name, factor in factors.items():
        out[name] = (out[name] * factor).astype(out[name].dtype)
    return out
```

```python
import concourse.bass as bass
from concourse import mybir
from contextlib import ExitStack

F32 = mybir.dt.float32
F16 = mybir.dt.float16
BF16 = mybir.dt.bfloat16
ACT = mybir.ActivationFunctionType
ALU = mybir.AluOpType

P = 128
B, N, F = 8, 2048, 128
KT = N // P
GC = 4
GT = GC * P
NQ = N // GT
G_ALL = B * NQ
H, HD, DS = 4, 64, 64
DI = H * HD
TAPS = 4
EPS = 1e-5
L_SCALE = 4096.0
X_SCALE = 1024.0
MASKED = -1e30
ATANH = [2.0000000078777487, 0.6666631593508168, 0.4002485372344133, 0.2796141883517147, 0.2817465726146668]
DT_OPS = 14


def over(ap, axis, n):
    a = ap.unsqueeze(axis)
    shape = list(a.shape)
    shape[axis] = n
    return a.to_broadcast(shape)


def gnn_mamba(nc, x, adj, gnn_W, W_in, conv_w, conv_b, dt_bias, A_log, D, norm_w, W_out, W_lin, b_lin, out):
    with ExitStack() as ctx:
        def sb(name, shape, dt=F32):
            return ctx.enter_context(nc.sbuf_tensor(name, shape, dt))

        def sem(name):
            return ctx.enter_context(nc.semaphore(name))

        lap = sb("lap", [P, KT * N])
        S_ = lap[:, :].rearrange("p (k n) -> p k n", k=KT)
        L_ = lap[:, :].bitcast(F16).rearrange("p (k q t n) -> p k q t n", k=KT, q=NQ, t=2)
        lnx = sb("lnx", [P, KT, 2, F], F16)
        xhat = sb("xhat", [P, KT, F])
        gT_xn = sb("gT_xn", [P, GT])
        x1 = sb("x1", [P, NQ, GC, F])
        xnT = sb("xnT", [P, GT])
        xraw = sb("xraw", [P, 2, TAPS - 1 + GT])
        ysq = xraw[:, :, :].rearrange("p a b -> p (a b)")[:, 0:2 * GT].rearrange("p (j t) -> p j t", j=2)
        halo = sb("halo", [P, 2, 3, TAPS - 1])
        xs = sb("xs", [P, 2, 3, GT])
        sz = sb("sz", [P, 2, 2, GT])
        CC = sb("CC", [P, GT])
        Lx = sb("Lx", [P, 2, H, P])
        CE = sb("CE", [P, 2, 2, P])
        xdtb = sb("xdtb", [P, 2, 2 * H * HD + 2 * DS])
        xdtp = xdtb[:, :, 0:2 * H * HD].rearrange("p a (h d) -> p a h d", h=H)
        Bp = xdtb[:, :, (2 * H - 1) * HD:]
        xdd = sb("xdd", [P, 2, 2, 2, HD])
        state = sb("state", [P, 2, 2, P])
        w_in = sb("w_in", [P, 2 * DI + 2 * DS + H])
        w_gnn = sb("w_gnn", [P, F])
        wc = sb("wc", [P, 2, F])
        ident = sb("ident", [P, P])
        upper = sb("upper", [P, P])
        onec = sb("onec", [P, 1])
        identb = sb("identb", [P, P], BF16)
        maskb = sb("maskb", [P, P], BF16)
        pick = sb("pick", [48, 16, HD], BF16)
        zero3 = sb("zero3", [P, 4])
        cw = sb("cw", [P, 3, TAPS])
        cb_ = sb("cb_", [P, 3])
        dcol = sb("dcol", [P, 2])
        nwc = sb("nwc", [P, 2])
        dtb = sb("dtb", [P, H])
        aexp = sb("aexp", [P, H])
        aneg = sb("aneg", [P, H])
        blin = sb("blin", [P, F])
        half = sb("half", [P, 16])
        mone = sb("mone", [P, 16])
        st1 = sb("st1", [P, GC, 6])
        mv1 = sb("mv1", [P, GC, 2])
        rs1 = sb("rs1", [P, GC])
        st2 = sb("st2", [P, GC, 6])
        mv2 = sb("mv2", [P, GC, 2])
        rs2 = sb("rs2", [P, GC])
        v_dt = sb("v_dt", [P, 16])
        nab = sb("nab", [P, 16])
        e_dt = sb("e_dt", [P, 16])
        ch = sb("ch", [P, 5, 16])
        dtv = sb("dtv", [P, 2, 16])
        dA = sb("dA", [P, 16])
        ncum = sb("ncum", [P, 2, 16])
        res = sb("res", [P, 16])
        parts = sb("parts", [P, 3, 16], BF16)
        cumT = sb("cumT", [48, 2, P], BF16)
        dcy = sb("dcy", [P, 2, H])
        dce = sb("dce", [P, 2, 2])
        ssm = sb("ssm", [P, GC])
        rms = sb("rms", [P, GC])

        diag = sz[:, 0, :, :].rearrange("p a b -> p (a b)")[:, 0:GT].rearrange("p (t n) -> p t n", t=GC)
        ring = xs[:, :, :, :].rearrange("p a j n -> p (a j) n")
        RING = 6
        ones = sz[:, 1, 0, 0:P]
        rsp = xnT[:, 0:KT * NQ].rearrange("p (k q) -> p k q", k=KT)
        rsum, cinv, negc, msk = (xnT[:, KT * (NQ + i):KT * (NQ + i + 1)] for i in range(4))
        wo = Lx[:, 0, 0:2, :]
        woT = Lx[:, 1, 0:2, :]
        wl = Lx[:, 0, 2, :]

        bank = [ctx.enter_context(nc.psum_tensor(f"bank{i}", [P, 512], F32)) for i in range(8)]
        p_gn, p_front, p_ip, p_diff, p_e, p_y = bank[0], bank[1], bank[2], bank[3], bank[4], bank[5]
        p_tg = [bank[6], bank[7]]
        p_cumT = p_front[0:48, 64:128].bitcast(BF16)

        adj_in = [sem(f"adj_in{i}") for i in range(KT)]
        w_landed = sem("w_landed")
        consts_pool = sem("consts_pool")
        consts_dve = sem("consts_dve")
        zeroed = sem("zeroed")
        unread = sem("unread")
        aexp_done, aneg_done = sem("aexp_done"), sem("aneg_done")
        wot_mm, wot_done, wc_mm, wc_done = sem("wot_mm"), sem("wot_done"), sem("wc_mm"), sem("wc_done")
        sym_mm, sym_add = sem("sym_mm"), sem("sym_add")
        relu_done, rsum_done, cinv_done = sem("relu_done"), sem("rsum_done"), sem("cinv_done")
        diag_done, cbc_mm = sem("diag_done"), sem("cbc_mm")
        lt_done, ld_done, lhi_done = sem("lt_done"), sem("ld_done"), sem("lhi_done")
        llo_dve, llo_pool = sem("llo_dve"), sem("llo_pool")

        xh_in = [sem("xh_in0"), sem("xh_in1")]
        st1_done, mv1_done, rs1_done, xh_done = sem("st1_done"), sem("mv1_done"), sem("rs1_done"), sem("xh_done")
        hi_done, lo_done = sem("hi_done"), sem("lo_done")
        rs1_var = sem("rs1_var")
        x_in = [sem("x_in0"), sem("x_in1")]
        gn_mm, gT_done = sem("gn_mm"), sem("gT_done")
        w_mm, x1_done, st2_done, mv2_done = sem("w_mm"), sem("x1_done"), sem("st2_done"), sem("mv2_done")
        rs2_var, rs2_done, xn_done, xb_done = sem("rs2_var"), sem("rs2_done"), sem("xn_done"), sem("xb_done")
        t_mm, xnT_done = sem("t_mm"), sem("xnT_done")
        dt_mm, v_done, nab_done, e_done = sem("dt_mm"), sem("v_done"), sem("nab_done"), sem("e_done")
        chain, dA_done = sem("chain"), sem("dA_done")
        cum_mm, ncum_done = sem("cum_mm"), sem("ncum_done")
        split, parts_done, parts_mm, cumT_done = sem("split"), sem("parts_done"), sem("parts_mm"), sem("cumT_done")
        ip_mm, ip_free = sem("ip_mm"), sem("ip_free")
        tap, conv_done, silu_done = sem("tap"), sem("conv_done"), sem("silu_done")
        cc_in = sem("cc_in")
        g_mm, diff_mm, e_mm, mid_mm = sem("g_mm"), sem("diff_mm"), sem("e_mm"), sem("mid_mm")
        e_exp, l_exp = sem("e_exp"), sem("l_exp")
        dcy_done, ce_done, xdd_done = sem("dcy_done"), sem("ce_done"), sem("xdd_done")
        st_zero, xdt_done, m_done, yst_done = sem("st_zero"), sem("xdt_done"), sem("m_done"), sem("yst_done")
        gate_done, sq_done, ss_mm, ss_done = sem("gate_done"), sem("sq_done"), sem("ss_mm"), sem("ss_done")
        rms_done, out_mm, out_done = sem("rms_done"), sem("out_mm"), sem("out_done")
        stored = [sem("stored0"), sem("stored1")]

        def wait(eng, s, value):
            if isinstance(value, int) and value <= 0:
                return
            eng.wait_ge(s, value)

        def wait_apart(eng, s, value):
            wait(eng, s, value)
            if not isinstance(value, int):
                eng.sem_inc(unread, 1)

        def every_step(eng, step):
            for q in range(NQ):
                step(0, q, True, q >= 1, q >= 2, q >= 3)
            with eng.Fori(1, B - 1) as b:
                for q in range(NQ):
                    step(b, q, True, True, True, True)
            for q in range(NQ):
                step(B - 1, q, True, True, True, True)
            for q in range(3):
                step(B, q, False, q < 1, q < 2, True)

        sym_items = []
        for j in range(KT):
            for i0 in range(0, j, 4):
                n = min(4, j - i0)
                sym_items += [(j, i0, n, True), (j, i0, n, False)]
            sym_items.append((j, j, 1, True))
        sym_after = {j: max(m for m, it in enumerate(sym_items) if it[0] == j) + 1 for j in range(KT)}
        relu_items = [(k, q) for last in range(3, KT, 4) for k in range(last + 1) for q in range(NQ)
                      if max(k, 4 * q + 3) <= last and max(k, 4 * q + 3) > last - 4]
        l_items = [(k, q) for q in range(NQ) for k in range(KT)]

        def on_pool(m):
            return m % 3 == 2

        def x_tiles(t, b, q):
            return t[b, q * GT:(q + 1) * GT, :].rearrange("(t p) f -> p t f", p=P)

        def b_and_q(b, q, back):
            return (b, q - back) if q >= back else (b - 1, q - back + NQ)

        def of_parity(b, q, back):
            return 2 * b + (q - back) // 2 + 1

        block = ctx.enter_context(nc.Block())

        @block.sync
        def _(sp):
            a_rows = adj.rearrange("(k p) n -> k p n", p=P)
            for k in range(KT):
                sp.dma_start(S_[:, k, :], a_rows[k]).then_inc(adj_in[k], 16)
                if k == 3:
                    small = [
                        (w_in[:, :], W_in), (w_gnn[:, :], gnn_W), (wl, W_lin),
                        (wo, W_out.rearrange("(j c) k -> c j k", c=P)),
                        (cw[:, :, :], conv_w.rearrange("(j c) k -> c j k", c=P)),
                        (cb_[:, :], conv_b.rearrange("(j c) -> c j", c=P)),
                        (nwc[:, :], norm_w.rearrange("(j c) -> c j", c=P)),
                        (dtb[:, :], dt_bias.partition_broadcast(P)),
                        (aexp[:, :], A_log.partition_broadcast(P)),
                        (blin[:, :], b_lin.partition_broadcast(P)),
                    ]
                    for hh in range(2):
                        small.append((dcol[hh * HD:(hh + 1) * HD, :],
                                      D.rearrange("(j h) -> h j", h=2)[hh].partition_broadcast(HD)))
                    for dst, src in small:
                        sp.dma_start(dst, src, allow_slow_non_contiguous=True).then_inc(w_landed, 16)
            for q in range(NQ):
                if q >= 2:
                    sp.wait_ge(xh_in[q % 2], 16)
                sp.dma_start(xhat[:, q * GC:(q + 1) * GC, :], x_tiles(x, 0, q)).then_inc(xh_in[q % 2], 16)

            def step(b, q, gn, ap, bk, tl):
                s = b * NQ + q
                if gn:
                    wait(sp, stored[q % 2], 16 * of_parity(b, q, 4))
                    sp.dma_start(x1[:, q, :, :], x_tiles(x, b, q)).then_inc(x_in[q % 2], 16)
                    if not isinstance(b, int) or b < B - 1:
                        sp.wait_ge(lo_done, 4 * b + 4)
                        sp.wait_ge(hi_done, 4 * b + 4)
                        sp.dma_start(xhat[:, q * GC:(q + 1) * GC, :],
                                     x_tiles(x, b + 1, q)).then_inc(xh_in[q % 2], 16)
                if tl:
                    bt, qt = b_and_q(b, q, 3)
                    sp.wait_ge(out_done, s - 2)
                    sp.dma_start(x_tiles(out, bt, qt), x1[:, qt, :, :]).then_inc(stored[qt % 2], 16)
                if ap:
                    g, pr = s - 1, (q - 1) % 2
                    sp.wait_ge(silu_done, 4 * g + 1)
                    wait(sp, ce_done, 4 * g)
                    wait(sp, g_mm, 4 * g)
                    for hh in range(2):
                        sp.dma_start(CC[hh * DS:(hh + 1) * DS, :], xs[DS:2 * DS, pr, 2, :]).then_inc(cc_in, 16)

            every_step(sp, step)
            sp.wait_ge(stored[0], 16 * G_ALL // 2)
            sp.wait_ge(stored[1], 16 * G_ALL // 2)

        @block.gpsimd
        def _(pool):
            g_ = nc.gpsimd
            g_.memset(ident[:, :], 0.0)
            g_.memset(upper[:, :], 1.0)
            g_.memset(maskb[:, :], 0.0)
            g_.memset(pick[:, :, :], 0.0)
            g_.memset(half[:, :], -0.5)
            g_.memset(mone[:, :], -1.0)
            g_.memset(zero3[:, :], 0.0)
            g_.memset(onec[:, :], 1.0)
            g_.memset(ones, 1.0).then_inc(zeroed, 1)
            pool.wait_ge(zeroed, 1)
            g_.affine_select(out=ident[:, :], in_=ident[:, :], compare_op=ALU.not_equal, fill=1.0, base=0,
                             pattern=[[-1, P]], channel_multiplier=1).then_inc(zeroed, 1)
            g_.affine_select(out=upper[:, :], in_=upper[:, :], compare_op=ALU.is_ge, fill=0.0, base=0,
                             pattern=[[1, P]], channel_multiplier=-1)
            g_.affine_select(out=maskb[:, :], in_=maskb[:, :], compare_op=ALU.is_ge, fill=MASKED, base=0,
                             pattern=[[1, P]], channel_multiplier=-1)
            for part in range(3):
                g_.affine_select(out=pick[:, :, :], in_=pick[:, :, :], compare_op=ALU.not_equal, fill=-1.0,
                                 base=-16 * part, pattern=[[-1, 16], [0, HD]], channel_multiplier=1).then_inc(zeroed, 1)
                pool.wait_ge(zeroed, 3 + part)
            g_.tensor_copy(identb[:, :], ident[:, :])
            g_.memset(xdtb[:, :, :], 0.0)
            g_.memset(state[:, :, :, :], 0.0).then_inc(consts_pool, 1)

            def rstd1(n):
                wait_apart(pool, mv1_done, n + 1)
                wait_apart(pool, xh_done, n)
                g_.tensor_scalar(rs1[:, :], mv1[:, :, 1], EPS, None, ALU.add).then_inc(rs1_var, 1)
                pool.wait_ge(rs1_var, n + 1)
                g_.tensor_tensor(rs1[:, :], rs1[:, :], half[:, 0:GC], ALU.pow).then_inc(rs1_done, 1)

            for n in range(NQ):
                rstd1(n)

            pool.wait_ge(rsum_done, 1)
            g_.tensor_scalar(msk[:, :], rsum[:, :], 0.0, None, ALU.is_gt).then_inc(cinv_done, 1)
            g_.tensor_scalar(cinv[:, :], rsum[:, :], 1e-37, None, ALU.max).then_inc(cinv_done, 1)
            pool.wait_ge(cinv_done, 2)
            g_.tensor_tensor(cinv[:, :], cinv[:, :], half[:, :], ALU.pow).then_inc(cinv_done, 1)
            pool.wait_ge(cinv_done, 3)
            g_.tensor_tensor(cinv[:, :], cinv[:, :], msk[:, :], ALU.mult).then_inc(cinv_done, 1)
            pool.wait_ge(cinv_done, 4)
            g_.tensor_scalar(negc[:, :], cinv[:, :], -L_SCALE, None, ALU.mult).then_inc(cinv_done, 1)
            for m, (k, q) in enumerate(l_items):
                if on_pool(m):
                    pool.wait_ge(lhi_done, m + 1)
                    g_.tensor_tensor(L_[:, k, q, 1, :], ring[:, m % RING, :], L_[:, k, q, 0, :],
                                     ALU.subtract).then_inc(llo_pool, 1)

            def chunk_decay_and_ce(h, c):
                cb = c % 2
                pool.wait_ge(l_exp, 4 * h + c + 1)
                pool.wait_ge(e_exp, 4 * h + c + 1)
                wait_apart(pool, yst_done, 4 * h + c - 1)
                g_.tensor_copy(dce[:, cb, :], CE[:, cb, :, P - 1])
                g_.tensor_copy(dcy[:, cb, :], Lx[:, cb, :, P - 1]).then_inc(dcy_done, 1)
                if c == 0:
                    pool.wait_ge(cc_in, 32 * h + 32)
                pool.wait_ge(dcy_done, 4 * h + c + 1)
                g_.tensor_tensor(CE[:, cb, :, :], CE[:, cb, :, :],
                                 over(CC[:, c * P:(c + 1) * P], 1, 2), ALU.mult).then_inc(ce_done, 1)

            def chunk_xdd(h, c):
                cb = c % 2
                pool.wait_ge(xdt_done, 4 * h + c + 1)
                pool.wait_ge(dcy_done, 4 * h + c + 1)
                wait(pool, mid_mm, 4 * h + c - 1)
                g_.tensor_tensor(xdd[:, cb, :, :, :].rearrange("p h j d -> p j h d"),
                                 xdtp[:, cb, :, 0:HD].rearrange("p (j h) d -> p j h d", h=2),
                                 over(dcy[:, cb, :].rearrange("p (j h) -> p j h", h=2), 3, HD),
                                 ALU.mult).then_inc(xdd_done, 1)

            def softplus(g, pr):
                n = [0]

                def link(ins):
                    n[0] += 1
                    ins.then_inc(chain, 1)
                    wait_apart(pool, chain, DT_OPS * g + n[0])
                pool.wait_ge(v_done, g + 1)
                wait_apart(pool, e_done, g + 1)
                m, den, z, z2, poly = (ch[:, i, :] for i in range(5))
                link(g_.tensor_scalar(m, v_dt[:, :], 0.0, None, ALU.max))
                link(g_.tensor_scalar(den, e_dt[:, :], 2.0, None, ALU.add))
                link(g_.tensor_tensor(den, den, mone[:, :], ALU.pow))
                link(g_.tensor_tensor(z, e_dt[:, :], den, ALU.mult))
                link(g_.tensor_tensor(z2, z, z, ALU.mult))
                link(g_.tensor_scalar(poly, z2, ATANH[4], ATANH[3], ALU.mult, ALU.add))
                for a in (2, 1, 0):
                    link(g_.tensor_tensor(poly, poly, z2, ALU.mult))
                    link(g_.tensor_scalar(poly, poly, ATANH[a], None, ALU.add))
                link(g_.tensor_tensor(poly, poly, z, ALU.mult))
                link(g_.tensor_tensor(dtv[:, pr, :], poly, m, ALU.add))
                assert n[0] == DT_OPS
                g_.tensor_tensor(dA[:, :].rearrange("p (c h) -> p c h", h=H),
                                 dtv[:, pr, :].rearrange("p (c h) -> p c h", h=H),
                                 over(aneg[:, :], 1, GC), ALU.mult).then_inc(dA_done, 1)

            def split_cum(g, pr):
                pool.wait_ge(ncum_done, g + 1)
                wait_apart(pool, parts_mm, g)
                nc_ = ncum[:, pr, :]
                g_.tensor_copy(parts[:, 0, :], nc_).then_inc(split, 1)
                pool.wait_ge(split, 3 * g + 1)
                g_.tensor_tensor(res[:, :], nc_, parts[:, 0, :], ALU.subtract).then_inc(split, 1)
                wait_apart(pool, split, 3 * g + 2)
                g_.tensor_copy(parts[:, 1, :], res[:, :]).then_inc(split, 1)
                pool.wait_ge(split, 3 * g + 3)
                g_.tensor_tensor(parts[:, 2, :], res[:, :], parts[:, 1, :], ALU.subtract).then_inc(parts_done, 1)

            def step(b, q, gn, ap, bk, tl):
                s = b * NQ + q
                g, h, t = s - 1, s - 2, s - 3
                pa, pb = (q - 1) % 2, q % 2
                last = isinstance(b, int) and b >= B - 1
                if bk:
                    chunk_decay_and_ce(h, 0)
                if ap:
                    wait_apart(pool, mv2_done, g + 1)
                    g_.tensor_scalar(rs2[:, :], mv2[:, :, 1], EPS, None, ALU.add).then_inc(rs2_var, 1)
                    pool.wait_ge(rs2_var, g + 1)
                    g_.tensor_tensor(rs2[:, :], rs2[:, :], half[:, 0:GC], ALU.pow).then_inc(rs2_done, 1)
                if bk:
                    chunk_xdd(h, 0)
                if tl:
                    pool.wait_ge(ss_done, t + 1)
                    wait(pool, out_done, t)
                    g_.tensor_tensor(rms[:, :], ssm[:, :], half[:, 0:GC], ALU.pow).then_inc(rms_done, 1)
                if bk:
                    chunk_decay_and_ce(h, 1)
                    chunk_xdd(h, 1)
                if ap:
                    qa = (q - 1) % 4
                    pool.wait_ge(xn_done, g + 1)
                    g_.tensor_tensor(x1[:, qa, :, :], x1[:, qa, :, :], over(blin[:, :], 1, GC),
                                     ALU.add).then_inc(xb_done, 1)
                    softplus(g, pa)
                if gn and not last:
                    rstd1(s + NQ)
                if bk:
                    chunk_decay_and_ce(h, 2)
                    chunk_xdd(h, 2)
                if ap:
                    split_cum(g, pa)
                if bk:
                    chunk_decay_and_ce(h, 3)
                    chunk_xdd(h, 3)

            every_step(pool, step)

        @block.scalar
        def _(act):
            a_ = nc.scalar
            act.wait_ge(w_landed, 16 * 12)
            a_.activation(aexp[:, :], aexp[:, :], ACT.Exp).then_inc(aexp_done, 1)
            act.wait_ge(wot_mm, 1)
            a_.activation(woT, p_front[:, 0:2 * P].rearrange("p (j c) -> p j c", j=2), ACT.Copy).then_inc(wot_done, 1)

            done = 0
            for k, q in relu_items:
                need = sym_after[max(k, 4 * q + 3)]
                if need > done:
                    act.wait_ge(sym_add, need)
                    done = need
                blk = S_[:, k, q * GT:(q + 1) * GT]
                a_.activation(blk, blk, ACT.Relu, accum_out=rsp[:, k, q:q + 1]).then_inc(relu_done, 1)

            def split_hi(kk, count):
                act.wait_ge(xh_done, count)
                a_.activation(lnx[:, 4 * kk:4 * kk + 4, 0, :], xhat[:, 4 * kk:4 * kk + 4, :],
                              ACT.Copy, scale=X_SCALE).then_inc(hi_done, 1)

            for kk in range(4):
                split_hi(kk, kk + 1)
            for m, (k, q) in enumerate(l_items):
                act.wait_ge(lt_done, m + 1)
                if k // 4 == q:
                    act.wait_ge(ld_done, k + 1)
                a_.activation(L_[:, k, q, 0, :], ring[:, m % RING, :], ACT.Copy).then_inc(lhi_done, 1)

            def exps(h, c, pr):
                cb = c % 2
                wait(act, mid_mm, 4 * h + c - 1)
                act.wait_ge(e_mm, 4 * h + c + 1)
                a_.activation(CE[:, cb, :, :], p_e[:, 0:2 * P].rearrange("p (j l) -> p j l", j=2),
                              ACT.Exp).then_inc(e_exp, 1)
                act.wait_ge(diff_mm, 4 * h + c + 1)
                act.wait_ge(ncum_done, h + 1)
                for hh in range(H):
                    last = a_.activation(Lx[:, cb, hh, :], p_diff[:, hh * P:(hh + 1) * P], ACT.Exp,
                                         bias=ncum[:, pr, c * H + hh:c * H + hh + 1])
                last.then_inc(l_exp, 1)

            def conv_in(g, i, j, pr, first):
                n = 3 * g + i
                buf = (pr + i) % 2
                act.wait_ge(ip_mm, 5 * g + i + 1)
                wait(act, conv_done, n - 1)
                if i == 0:
                    wait(act, ss_mm, g - 1)
                    wait(act, out_mm, g - 1)
                wait(act, ip_free, 5 * (g - 1) + i + 1)
                a_.activation(xraw[:, buf, 0:3], zero3[:, 0:3] if first else halo[:, 1 - pr, j, :], ACT.Copy)
                a_.activation(xraw[:, buf, 3:3 + GT], p_ip[:, :], ACT.Copy)
                a_.activation(halo[:, pr, j, :], p_ip[:, GT - 3:GT], ACT.Copy)
                a_.activation(xs[:, pr, j, :], p_ip[:, :], ACT.Identity, bias=cb_[:, j:j + 1],
                              scale=cw[:, j, 3:4]).then_inc(ip_free, 1)

            def step(b, q, gn, ap, bk, tl):
                s = b * NQ + q
                g, h, t = s - 1, s - 2, s - 3
                pa, pb, pt = (q - 1) % 2, q % 2, (q - 3) % 2
                last = isinstance(b, int) and b >= B - 1
                if tl:
                    act.wait_ge(gate_done, t + 1)
                    a_.activation(ysq, xs[:, pt, 0:2, :], ACT.Square).then_inc(sq_done, 1)
                if bk:
                    exps(h, 0, pb)
                if tl:
                    act.wait_ge(ss_mm, t + 1)
                    wait(act, rms_done, t)
                    a_.activation(ssm[:, :], p_y[:, 384:384 + GC], ACT.Copy, scale=1.0 / DI,
                                  bias=EPS).then_inc(ss_done, 1)
                if bk:
                    exps(h, 1, pb)
                if ap:
                    act.wait_ge(t_mm, g + 1)
                    wait(act, ip_mm, 5 * g)
                    a_.activation(xnT[:, :], p_front[:, :], ACT.Copy).then_inc(xnT_done, 1)
                    act.wait_ge(nab_done, g + 1)
                    a_.activation(e_dt[:, :], nab[:, :], ACT.Exp).then_inc(e_done, 1)
                    conv_in(g, 0, 2, pa, (q - 1) % 4 == 0)
                if gn and q == NQ - 1 and not last:
                    act.wait_ge(gn_mm, 4 * s + 1)
                    split_hi(0, 4 * (b + 1) + 1)
                if bk:
                    exps(h, 2, pb)
                if ap:
                    conv_in(g, 1, 0, pa, (q - 1) % 4 == 0)
                    act.wait_ge(cum_mm, g + 1)
                    a_.activation(ncum[:, pa, :], p_front[:, 32:48], ACT.Copy, scale=-1.0).then_inc(ncum_done, 1)
                if gn and q == NQ - 1 and not last:
                    act.wait_ge(gn_mm, 4 * s + 2)
                    split_hi(1, 4 * (b + 1) + 2)
                if bk:
                    exps(h, 3, pb)
                if ap:
                    conv_in(g, 2, 1, pa, (q - 1) % 4 == 0)
                    act.wait_ge(parts_mm, g + 1)
                    a_.activation(cumT[:, pa, :], p_cumT, ACT.Copy).then_inc(cumT_done, 1)
                if gn and q == NQ - 1 and not last:
                    act.wait_ge(gn_mm, 4 * s + 3)
                    split_hi(2, 4 * (b + 1) + 3)
                if ap:
                    act.wait_ge(ip_mm, 5 * g + 4)
                    wait(act, gate_done, g - 1)
                    a_.activation(sz[:, pa, 0, :], p_ip[:, :], ACT.Copy).then_inc(ip_free, 1)
                if gn:
                    act.wait_ge(gn_mm, 4 * s + 4)
                    wait(act, t_mm, s)
                    a_.activation(gT_xn[:, :], p_gn[:, :], ACT.Copy,
                                  scale=1.0 / (L_SCALE * X_SCALE)).then_inc(gT_done, 1)
                    if q == NQ - 1 and not last:
                        split_hi(3, 4 * (b + 1) + 4)
                if ap:
                    act.wait_ge(ip_mm, 5 * g + 5)
                    a_.activation(sz[:, pa, 1, :], p_ip[:, :], ACT.Copy).then_inc(ip_free, 1)
                    for i, j in enumerate((2, 0, 1)):
                        act.wait_ge(conv_done, 3 * g + i + 1)
                        a_.activation(xs[:, pa, j, :], xs[:, pa, j, :], ACT.Silu).then_inc(silu_done, 1)
                    act.wait_ge(ip_free, 5 * g + 5)
                    a_.activation(sz[:, pa, :, :], sz[:, pa, :, :], ACT.Silu).then_inc(silu_done, 1)

            every_step(act, step)

        @block.vector
        def _(dve):
            v_ = nc.vector
            v_.memset(dce[:, :, :], 0.0)

            for m, (j, i0, n, row) in enumerate(sym_items):
                dve.wait_ge(sym_mm, m + (2 if row and j != i0 else 1))
                dst = S_[:, j, i0 * P:(i0 + n) * P].rearrange("p (i n) -> p i n", i=n) if row \
                    else S_[:, i0:i0 + n, j * P:(j + 1) * P]
                v_.tensor_tensor(dst, dst, bank[m % 8][:, 0:n * P].rearrange("p (i n) -> p i n", i=n),
                                 ALU.add).then_inc(sym_add, 1)
                if m == 12:
                    dve.wait_ge(aexp_done, 1)
                    v_.tensor_scalar(aneg[:, :], aexp[:, :], -1.0, None, ALU.mult).then_inc(aneg_done, 1)

            def norm1(n, q):
                dve.wait_ge(rs1_done, n + 1)
                for c in range(GC):
                    xt = xhat[:, q * GC + c, :]
                    last = v_.tensor_scalar(xt, xt, mv1[:, c, 0:1], rs1[:, c:c + 1], ALU.subtract, ALU.mult)
                last.then_inc(xh_done, 1)

            def stats1(n, q, nth):
                dve.wait_ge(xh_in[q % 2], 16 * nth)
                for c in range(GC):
                    last = v_.bn_stats(st1[:, c, :], xhat[:, q * GC + c, :])
                last.then_inc(st1_done, 1)

            def aggr1(n):
                dve.wait_ge(st1_done, n + 1)
                wait_apart(dve, xh_done, n)
                for c in range(GC):
                    last = v_.bn_aggr(mv1[:, c, :], st1[:, c, :])
                last.then_inc(mv1_done, 1)

            def split_lo(kk, count):
                dve.wait_ge(hi_done, count)
                v_.scalar_tensor_tensor(lnx[:, 4 * kk:4 * kk + 4, 1, :], xhat[:, 4 * kk:4 * kk + 4, :], X_SCALE,
                                        lnx[:, 4 * kk:4 * kk + 4, 0, :], ALU.mult, ALU.subtract).then_inc(lo_done, 1)

            for q in range(NQ):
                stats1(q, q, q // 2 + 1)
                aggr1(q)
                norm1(q, q)
                split_lo(q, q + 1)

            dve.wait_ge(wc_mm, 1)
            for j in range(2):
                last = v_.tensor_scalar(wc[:, j, :], p_e[:, j * P:(j + 1) * P], nwc[:, j:j + 1], None, ALU.mult)
            last.then_inc(wc_done, 1)

            dve.wait_ge(relu_done, KT * NQ)
            v_.tensor_reduce(out=rsum[:, :], in_=rsp[:, :, :], axis=mybir.AxisListType.X,
                             op=ALU.add).then_inc(rsum_done, 1)
            dve.wait_ge(cinv_done, 5)
            for q in range(NQ):
                wait(dve, cbc_mm, q)
                v_.tensor_tensor(diag, over(ident[:, :], 1, GC), over(cinv[:, q * GC:(q + 1) * GC], 2, P),
                                 ALU.mult).then_inc(diag_done, 1)
            lo_mine = 0

            def lap_lo(m):
                k, q = l_items[m]
                dve.wait_ge(lhi_done, m + 1)
                v_.tensor_tensor(L_[:, k, q, 1, :], ring[:, m % RING, :], L_[:, k, q, 0, :],
                                 ALU.subtract).then_inc(llo_dve, 1)
            LAG = 3
            for m, (k, q) in enumerate(l_items):
                if m >= RING:
                    if on_pool(m - RING):
                        dve.wait_ge(llo_pool, sum(on_pool(i) for i in range(m - RING + 1)))
                    else:
                        dve.wait_ge(llo_dve, sum(not on_pool(i) for i in range(m - RING + 1)))
                if k == 0:
                    dve.wait_ge(cbc_mm, q + 1)
                v_.scalar_tensor_tensor(ring[:, m % RING, :], S_[:, k, q * GT:(q + 1) * GT], negc[:, k:k + 1],
                                        bank[q][:, :], ALU.mult, ALU.mult).then_inc(lt_done, 1)
                if k // 4 == q:
                    dve.wait_ge(lt_done, m + 1)
                    dg = ring[:, m % RING, (k % 4) * P:(k % 4 + 1) * P]
                    v_.scalar_tensor_tensor(dg, ident[:, :], L_SCALE, dg, ALU.mult, ALU.add).then_inc(ld_done, 1)
                if m >= LAG and not on_pool(m - LAG):
                    lap_lo(m - LAG)
            for m in range(len(l_items) - LAG, len(l_items)):
                if not on_pool(m):
                    lap_lo(m)

            def pre(h, c, pr, first):
                cb = c % 2
                tg = p_tg[cb]
                if first and c == 0:
                    wait(dve, yst_done, 4 * h)
                    v_.memset(state[:, 0, :, :], 0.0)
                dve.wait_ge(g_mm, 4 * h + c + 1)
                wait(dve, mid_mm, 4 * h + c - 1)
                wait(dve, xdd_done, 4 * h + c - 1)
                v_.tensor_tensor(xdtp[:, cb, :, 0:HD], tg[:, 0:DI].rearrange("p (h d) -> p h d", h=H),
                                 over(dtv[:, pr, c * H:(c + 1) * H], 2, HD), ALU.mult).then_inc(xdt_done, 1)
                v_.tensor_copy(Bp[:, cb, DS:2 * DS], tg[:, DI:DI + DS])
                dve.wait_ge(dcy_done, 4 * h + c + 1)
                v_.tensor_tensor(Lx[:, cb, :, :], over(tg[:, 320:448], 1, H), Lx[:, cb, :, :],
                                 ALU.mult).then_inc(m_done, 1)

            def post(h, c, pr):
                cb = c % 2
                dve.wait_ge(mid_mm, 4 * h + c + 1)
                for j in range(2):
                    xc = xs[:, pr, j, c * P:(c + 1) * P]
                    v_.scalar_tensor_tensor(xc, xc, dcol[:, j:j + 1], p_y[:, j * P:(j + 1) * P], ALU.mult, ALU.add)
                for j in range(2):
                    for hh in range(2):
                        rows = slice(hh * DS, (hh + 1) * DS)
                        last = v_.scalar_tensor_tensor(
                            state[rows, 1 - cb, j, hh * HD:(hh + 1) * HD], state[rows, cb, j, hh * HD:(hh + 1) * HD],
                            dce[rows, cb, j:j + 1], p_y[rows, 2 * P + j * HD:2 * P + (j + 1) * HD], ALU.mult, ALU.add)
                last.then_inc(yst_done, 1)

            def conv(g, i, j, pr):
                buf = (pr + i) % 2
                dve.wait_ge(ip_free, 5 * g + i + 1)
                acc = xs[:, pr, j, :]
                for k in (2, 1, 0):
                    if k < 2:
                        dve.wait_ge(tap, 6 * g + 2 * i + 2 - k)
                    ins = v_.scalar_tensor_tensor(acc, xraw[:, buf, k:k + GT], cw[:, j, k:k + 1], acc,
                                                  ALU.mult, ALU.add)
                    ins.then_inc(tap if k else conv_done, 1)

            def step(b, q, gn, ap, bk, tl):
                s = b * NQ + q
                g, h, t = s - 1, s - 2, s - 3
                qa, qt = (q - 1) % 4, (q - 3) % 4
                pa, pb = (q - 1) % 2, q % 2
                first = (q - 2) % 4 == 0
                last = isinstance(b, int) and b >= B - 1
                ln1 = gn and not last
                if ap:
                    dve.wait_ge(w_mm, g + 1)
                    dve.wait_ge(x_in[pa], 16 * of_parity(b, q, 1))
                    xt = x1[:, qa, :, :]
                    v_.scalar_tensor_tensor(xt, p_front[:, :].rearrange("p (c f) -> p c f", c=GC), 0.0, xt,
                                            ALU.max, ALU.add).then_inc(x1_done, 1)
                if bk:
                    pre(h, 0, pb, first)
                if ap:
                    dve.wait_ge(x1_done, g + 1)
                    for c in range(GC):
                        ins = v_.bn_stats(st2[:, c, :], x1[:, qa, c, :])
                    ins.then_inc(st2_done, 1)
                    wait_apart(dve, st2_done, g + 1)
                    for c in range(GC):
                        ins = v_.bn_aggr(mv2[:, c, :], st2[:, c, :])
                    ins.then_inc(mv2_done, 1)
                if bk:
                    pre(h, 1, pb, first)
                if ap:
                    dve.wait_ge(rs2_done, g + 1)
                    for c in range(GC):
                        ins = v_.tensor_scalar(gT_xn[:, c * P:(c + 1) * P], x1[:, qa, c, :], mv2[:, c, 0:1],
                                               rs2[:, c:c + 1], ALU.subtract, ALU.mult)
                    ins.then_inc(xn_done, 1)
                if bk:
                    post(h, 0, pb)
                if tl:
                    dve.wait_ge(out_mm, t + 1)
                    dve.wait_ge(rms_done, t + 1)
                    dve.wait_ge(xb_done, t + 1)
                    for c in range(GC):
                        xt = x1[:, qt, c, :]
                        ins = v_.scalar_tensor_tensor(xt, p_ip[:, c * P:(c + 1) * P], rms[:, c:c + 1], xt,
                                                      ALU.mult, ALU.add)
                    ins.then_inc(out_done, 1)
                if ln1:
                    stats1(s + NQ, q, 2 * (b + 1) + q // 2 + 1)
                if ap:
                    dve.wait_ge(dt_mm, g + 1)
                    wait(dve, dA_done, g)
                    v_.tensor_tensor(v_dt[:, :].rearrange("p (c h) -> p c h", h=H),
                                     p_front[:, 0:16].rearrange("p (c h) -> p c h", h=H),
                                     over(dtb[:, :], 1, GC), ALU.add).then_inc(v_done, 1)
                    if ln1:
                        aggr1(s + NQ)
                    dve.wait_ge(v_done, g + 1)
                    v_.scalar_tensor_tensor(nab[:, :], v_dt[:, :], -1.0, v_dt[:, :], ALU.mult, ALU.min).then_inc(nab_done, 1)
                elif ln1:
                    aggr1(s + NQ)
                if bk:
                    pre(h, 2, pb, first)
                if ap:
                    conv(g, 0, 2, pa)
                if bk:
                    post(h, 1, pb)
                if ln1:
                    norm1(s + NQ, q)
                    if q == NQ - 1:
                        split_lo(0, 4 * (b + 1) + 1)
                if bk:
                    pre(h, 3, pb, first)
                if ap:
                    conv(g, 1, 0, pa)
                if bk:
                    post(h, 2, pb)
                if ln1 and q == NQ - 1:
                    split_lo(1, 4 * (b + 1) + 2)
                if ap:
                    conv(g, 2, 1, pa)
                if ln1 and q == NQ - 1:
                    split_lo(2, 4 * (b + 1) + 3)
                if bk:
                    post(h, 3, pb)
                    dve.wait_ge(silu_done, 4 * h + 4)
                    dve.wait_ge(yst_done, 4 * h + 4)
                    v_.tensor_tensor(xs[:, pb, 0:2, :], xs[:, pb, 0:2, :], sz[:, pb, :, :],
                                     ALU.mult).then_inc(gate_done, 1)
                if ln1 and q == NQ - 1:
                    split_lo(3, 4 * (b + 1) + 4)

            every_step(dve, step)

        @block.tensor
        def _(pe):
            t_ = nc.tensor
            pe.wait_ge(consts_pool, 1)
            for m, (j, i0, n, row) in enumerate(sym_items):
                if m == 0 or sym_items[m - 1][0] != j:
                    pe.wait_ge(adj_in[j], 16)
                if m >= 8:
                    pe.wait_ge(sym_add, m - 7)
                for i in range(n):
                    src = S_[:, i0 + i, j * P:(j + 1) * P] if row else S_[:, j, (i0 + i) * P:(i0 + i + 1) * P]
                    last = t_.transpose(bank[m % 8][:, i * P:(i + 1) * P], src, ident[:, :])
                last.then_inc(sym_mm, 1)
            pe.wait_ge(sym_add, len(sym_items))
            pe.wait_ge(w_landed, 16 * 12)
            for j in range(2):
                last = t_.transpose(p_front[:, j * P:(j + 1) * P], wo[:, j, :], ident[:, :])
            last.then_inc(wot_mm, 1)
            pe.wait_ge(wot_done, 1)
            for j in range(2):
                last = t_.matmul(p_e[:, j * P:(j + 1) * P], woT[:, j, :], wl, start=True, stop=True)
            last.then_inc(wc_mm, 1)
            pe.wait_ge(wc_done, 1)
            for q in range(NQ):
                pe.wait_ge(diag_done, q + 1)
                t_.matmul(bank[q][:, :], ones, diag.rearrange("p t n -> p (t n)"), start=True,
                          stop=True).then_inc(cbc_mm, 1)
            pe.wait_ge(llo_dve, sum(not on_pool(m) for m in range(len(l_items))))
            pe.wait_ge(llo_pool, sum(on_pool(m) for m in range(len(l_items))))

            def laplacian(b, q, m0, m1):
                s = b * NQ + q
                for m in range(m0, m1):
                    k, term = m // 3, m % 3
                    if m == 0:
                        wait(pe, gT_done, s)
                    if q == 0 and m % 12 == 0:
                        pe.wait_ge(lo_done, 4 * b + m // 12 + 1)
                        pe.wait_ge(hi_done, 4 * b + m // 12 + 1)
                    ins = t_.matmul(p_gn[:, :], lnx[:, k, term // 2, :], L_[:, k, q, term % 2, :],
                                    start=(m == 0), stop=(m == 3 * KT - 1))
                    if m % 12 == 11:
                        ins.then_inc(gn_mm, 1)

            def chunk_in(h, c, pr):
                cb = c % 2
                tg = p_tg[cb]
                cs = slice(c * P, (c + 1) * P)
                rows = cumT[:, pr, :]
                pe.wait_ge(cumT_done, h + 1)
                wait(pe, e_exp, 4 * h + c)
                for j in range(2):
                    ins = t_.matmul(p_e[:, j * P:(j + 1) * P], pick[:, c * H + 2 * j:c * H + 2 * j + 2, :].rearrange("r h d -> r (h d)"),
                                    rows, start=True, stop=True)
                ins.then_inc(e_mm, 1)
                wait(pe, l_exp, 4 * h + c)
                t_.matmul(p_diff[:, :], identb[:, :], over(maskb[:, :], 1, H), start=True, stop=False)
                for hh in range(H):
                    ins = t_.matmul(p_diff[:, hh * P:(hh + 1) * P], over(pick[:, c * H + hh, 0], 1, P), rows,
                                    start=False, stop=(hh == H - 1))
                ins.then_inc(diff_mm, 1)
                if c == 0:
                    pe.wait_ge(silu_done, 4 * h + 3)
                    pe.wait_ge(cc_in, 32 * h + 32)
                wait(pe, m_done, 4 * h + c - 1)
                t_.transpose(tg[:, 0:P], xs[:, pr, 0, cs], ident[:, :])
                t_.transpose(tg[:, P:2 * P], xs[:, pr, 1, cs], ident[:, :])
                t_.transpose(tg[:, DI:DI + DS], xs[0:DS, pr, 2, cs], ident[0:DS, 0:DS])
                t_.matmul(tg[:, 320:448], xs[0:DS, pr, 2, cs], CC[0:DS, cs], start=True, stop=True).then_inc(g_mm, 1)

            def chunk_out(h, c, tl):
                cb = c % 2
                pe.wait_ge(m_done, 4 * h + c + 1)
                pe.wait_ge(ce_done, 4 * h + c + 1)
                wait(pe, yst_done, 4 * h + c)
                if c == 0 and tl:
                    pe.wait_ge(ss_done, h)
                for j in range(2):
                    y = p_y[:, j * P:(j + 1) * P]
                    xp = xdtb[:, cb, :]
                    t_.matmul(y, xp[:, 4 * j * HD:4 * j * HD + P], Lx[:, cb, 2 * j, :], start=True, stop=False)
                    t_.matmul(y, xp[:, (4 * j + 1) * HD:(4 * j + 1) * HD + P], Lx[:, cb, 2 * j + 1, :],
                              start=False, stop=False)
                    t_.matmul(y, state[:, cb, j, :], CE[:, cb, j, :], start=False, stop=True)
                pe.wait_ge(xdd_done, 4 * h + c + 1)
                for hh in range(2):
                    ins = t_.matmul(p_y[:, 2 * P:3 * P], Bp[:, cb, (1 - hh) * DS:(1 - hh) * DS + P],
                                    xdd[:, cb, hh, :, :].rearrange("p j d -> p (j d)"), start=(hh == 0), stop=(hh == 1))
                ins.then_inc(mid_mm, 1)

            def project(g, i):
                col = (DI + 2 * P, DI, DI + P, 0, P)[i]
                wait(pe, ip_free, 5 * g + i)
                if i == 0:
                    wait(pe, out_done, g - 1)
                t_.matmul(p_ip[:, :], w_in[:, col:col + P], xnT[:, :], start=True, stop=True).then_inc(ip_mm, 1)

            def step(b, q, gn, ap, bk, tl):
                s = b * NQ + q
                g, h, t = s - 1, s - 2, s - 3
                pa, pb, pt = (q - 1) % 2, q % 2, (q - 3) % 2
                if ap:
                    pe.wait_ge(gT_done, g + 1)
                    wait(pe, cumT_done, g)
                    for c in range(GC):
                        ins = t_.matmul(p_front[:, c * P:(c + 1) * P], gT_xn[:, c * P:(c + 1) * P], w_gnn[:, :],
                                        start=True, stop=True)
                    ins.then_inc(w_mm, 1)
                if gn:
                    laplacian(b, q, 0, 8)
                if bk:
                    chunk_in(h, 0, pb)
                if tl:
                    pe.wait_ge(sq_done, t + 1)
                    pe.wait_ge(yst_done, 4 * t + 4)
                    for c in range(GC):
                        for j in range(2):
                            ins = t_.matmul(p_y[:, 384 + c:385 + c], ysq[:, j, c * P:(c + 1) * P], onec[:, :],
                                            start=(j == 0), stop=(j == 1))
                    ins.then_inc(ss_mm, 1)
                if gn:
                    laplacian(b, q, 8, 12)
                if bk:
                    chunk_in(h, 1, pb)
                if tl:
                    wait(pe, ip_free, 5 * (t + 2) if not isinstance(t, int) else 5 * min(t + 2, G_ALL))
                    for c in range(GC):
                        for j in range(2):
                            ins = t_.matmul(p_ip[:, c * P:(c + 1) * P], xs[:, pt, j, c * P:(c + 1) * P], wc[:, j, :],
                                            start=(j == 0), stop=(j == 1))
                    ins.then_inc(out_mm, 1)
                if bk:
                    chunk_out(h, 0, tl)
                if gn:
                    laplacian(b, q, 12, 20)
                if ap:
                    pe.wait_ge(xn_done, g + 1)
                    for c in range(GC):
                        ins = t_.transpose(p_front[:, c * P:(c + 1) * P], gT_xn[:, c * P:(c + 1) * P], ident[:, :])
                    ins.then_inc(t_mm, 1)
                if gn:
                    laplacian(b, q, 20, 26)
                if ap:
                    pe.wait_ge(xnT_done, g + 1)
                    for c in range(GC):
                        ins = t_.matmul(p_front[:, c * H:(c + 1) * H], xnT[:, c * P:(c + 1) * P],
                                        w_in[:, 2 * DI + 2 * DS:2 * DI + 2 * DS + H], start=True, stop=True)
                    ins.then_inc(dt_mm, 1)
                    project(g, 0)
                if bk:
                    chunk_in(h, 2, pb)
                    chunk_out(h, 1, tl)
                if gn:
                    laplacian(b, q, 26, 31)
                if ap:
                    project(g, 1)
                if gn:
                    laplacian(b, q, 31, 35)
                if ap:
                    pe.wait_ge(dA_done, g + 1)
                    t_.matmul(p_front[:, 32:48], upper[:, :], dA[:, :], start=True, stop=True).then_inc(cum_mm, 1)
                if bk:
                    chunk_in(h, 3, pb)
                    chunk_out(h, 2, tl)
                if ap:
                    project(g, 2)
                if gn:
                    laplacian(b, q, 35, 40)
                if ap:
                    wait_apart(pe, parts_done, g + 1)
                    t_.transpose(p_cumT, parts[:, :, :].rearrange("p a b -> p (a b)"), identb[:, :]).then_inc(parts_mm, 1)
                if bk:
                    chunk_out(h, 3, tl)
                if ap:
                    project(g, 3)
                if gn:
                    laplacian(b, q, 40, 48)
                if ap:
                    project(g, 4)

            every_step(pe, step)


_INS = ["x", "adj", "L0_gnn_W", "L0_ffn_W_in", "L0_ffn_conv_w", "L0_ffn_conv_b", "L0_ffn_dt_bias", "L0_ffn_A_log",
        "L0_ffn_D", "L0_ffn_norm_w", "L0_ffn_W_out", "L0_ffn_W_lin", "L0_ffn_b_lin"]


def kernel(**inputs):
    import numpy as _np
    import concourse.bacc as _bacc
    from concourse import mybir as _mybir
    from concourse.bass_utils import run_bass_kernel_spmd as _run

    nc = _bacc.Bacc("TRN2", target_bir_lowering=False, num_devices=1)
    arrays, args = {}, []
    for name in _INS:
        a = _np.ascontiguousarray(inputs[name])
        arrays[f"in_{name}"] = a
        args.append(nc.dram_tensor(f"in_{name}", a.shape, _mybir.dt.from_np(a.dtype), kind="ExternalInput").ap())
    o = nc.dram_tensor("out", (B, N, F), F32, kind="ExternalOutput").ap()
    gnn_mamba(nc, *args, o)
    r = _run(nc, [arrays], core_ids=[0])
    return r.results[0]["out"]
```

```python
import concourse.bass as bass
from concourse import mybir
from contextlib import ExitStack

F32 = mybir.dt.float32
F16 = mybir.dt.float16
BF16 = mybir.dt.bfloat16
ACT = mybir.ActivationFunctionType
ALU = mybir.AluOpType

P = 128
B, N, F = 8, 2048, 128
KT = N // P
GC = 4
GT = GC * P
NQ = N // GT
G_ALL = B * NQ
H, HD, DS = 4, 64, 64
DI = H * HD
TAPS = 4
EPS = 1e-5
L_SCALE = 4096.0
X_SCALE = 1024.0
MASKED = -1e30
ATANH = [2.0000000078777487, 0.6666631593508168, 0.4002485372344133, 0.2796141883517147, 0.2817465726146668]
DT_OPS = 10


def over(ap, axis, n):
    a = ap.unsqueeze(axis)
    shape = list(a.shape)
    shape[axis] = n
    return a.to_broadcast(shape)


def gnn_mamba(nc, x, adj, gnn_W, W_in, conv_w, conv_b, dt_bias, A_log, D, norm_w, W_out, W_lin, b_lin, out):
    with ExitStack() as ctx:
        def sb(name, shape, dt=F32):
            return ctx.enter_context(nc.sbuf_tensor(name, shape, dt))

        def sem(name):
            return ctx.enter_context(nc.semaphore(name))

        lap = sb("lap", [P, KT * N])
        S_ = lap[:, :].rearrange("p (k n) -> p k n", k=KT)
        L_ = lap[:, :].bitcast(F16).rearrange("p (k q t n) -> p k q t n", k=KT, q=NQ, t=2)
        lnx = sb("lnx", [P, KT, 2, F], F16)
        xhat = sb("xhat", [P, KT, F])
        gT_xn = sb("gT_xn", [P, GT])
        x1 = sb("x1", [P, NQ, GC, F])
        xnT = sb("xnT", [P, GT])
        xraw = sb("xraw", [P, 2, TAPS - 1 + GT])
        ysq = xraw[:, :, :].rearrange("p a b -> p (a b)")[:, 0:2 * GT].rearrange("p (j t) -> p j t", j=2)
        halo = sb("halo", [P, 2, 3, TAPS - 1])
        xs = sb("xs", [P, 2, 3, GT])
        sz = sb("sz", [P, 2, 2, GT])
        CC = sb("CC", [P, GT])
        Lx = sb("Lx", [P, 2, H, P])
        CE = sb("CE", [P, 2, 2, P])
        xdtb = sb("xdtb", [P, 2, 2 * H * HD + 2 * DS])
        xdtp = xdtb[:, :, 0:2 * H * HD].rearrange("p a (h d) -> p a h d", h=H)
        Bp = xdtb[:, :, (2 * H - 1) * HD:]
        xdd = sb("xdd", [P, 2, 2, 2, HD])
        state = sb("state", [P, 2, 2, P])
        w_in = sb("w_in", [P, 2 * DI + 2 * DS + H])
        w_gnn = sb("w_gnn", [P, F])
        wc = sb("wc", [P, 2, F])
        ident = sb("ident", [P, P])
        upper = sb("upper", [P, P])
        onec = sb("onec", [P, 1])
        identb = sb("identb", [P, P], BF16)
        maskb = sb("maskb", [P, P], BF16)
        pick = sb("pick", [48, 16, HD], BF16)
        zero3 = sb("zero3", [P, 4])
        cw = sb("cw", [P, 3, TAPS])
        cb_ = sb("cb_", [P, 3])
        dcol = sb("dcol", [P, 2])
        nwc = sb("nwc", [P, 2])
        dtb = sb("dtb", [P, H])
        aexp = sb("aexp", [P, H])
        aneg = sb("aneg", [P, H])
        blin = sb("blin", [P, F])
        half = sb("half", [P, 16])
        negc = sb("negc", [P, KT])
        st1 = sb("st1", [P, GC, 6])
        mv1 = sb("mv1", [P, GC, 2])
        rs1 = sb("rs1", [P, GC])
        st2 = sb("st2", [P, GC, 6])
        mv2 = sb("mv2", [P, GC, 2])
        rs2 = sb("rs2", [P, GC])
        v_dt = sb("v_dt", [P, 16])
        nab = sb("nab", [P, 16])
        e_dt = sb("e_dt", [P, 16])
        ch = sb("ch", [P, 5, 16])
        dtv = sb("dtv", [P, 2, 16])
        dA = sb("dA", [P, 16])
        ncum = sb("ncum", [P, 2, 16])
        res = sb("res", [P, 16])
        parts = sb("parts", [P, 3, 16], BF16)
        cumT = sb("cumT", [48, 2, P], BF16)
        dcy = sb("dcy", [P, 2, H])
        dce = sb("dce", [P, 2, 2])
        ssm = sb("ssm", [P, GC])
        rms = sb("rms", [P, GC])

        diag = sz[:, 0, :, :].rearrange("p a (t n) -> p a t n", t=GC)
        ring = [xs[:, 1, 0, :], xs[:, 1, 1, :], xs[:, 1, 2, :], sz[:, 1, 0, :], sz[:, 1, 1, :],
                Lx[:, 1, :, :].rearrange("p h l -> p (h l)")]
        RING = len(ring)
        LAG = 3
        ones = xs[:, 0, 0, 0:P]
        rsp = xnT[:, 0:KT * NQ].rearrange("p (k q) -> p k q", k=KT)
        rsum, cinv, msk = (xnT[:, KT * (NQ + i):KT * (NQ + i + 1)] for i in range(3))
        wo = Lx[:, 0, 0:2, :]
        woT = Lx[:, 1, 0:2, :]
        wl = Lx[:, 0, 2, :]

        bank = [ctx.enter_context(nc.psum_tensor(f"bank{i}", [P, 512], F32)) for i in range(8)]
        p_gn, p_front, p_ip, p_diff, p_e, p_y = bank[0], bank[1], bank[2], bank[3], bank[4], bank[5]
        p_tg = [bank[6], bank[7]]
        p_col = [p_e, p_y, p_tg[0], p_tg[1]]
        p_cumT = p_front[0:48, 64:128].bitcast(BF16)

        adj_in = [sem(f"adj_in{i}") for i in range(KT)]
        w_landed = sem("w_landed")
        consts_pool = sem("consts_pool")
        consts_dve = sem("consts_dve")
        zeroed = sem("zeroed")
        unread = sem("unread")
        aexp_done, aneg_done = sem("aexp_done"), sem("aneg_done")
        wot_mm, wot_done, wc_mm, wc_done = sem("wot_mm"), sem("wot_done"), sem("wc_mm"), sem("wc_done")
        sym_mm, sym_add = sem("sym_mm"), sem("sym_add")
        relu_act, relu_dve, rsum_done, cinv_done = sem("relu_act"), sem("relu_dve"), sem("rsum_done"), sem("cinv_done")
        diag_done, cbc_mm = sem("diag_done"), sem("cbc_mm")
        lt_done, ld_done, lhi_done = sem("lt_done"), sem("ld_done"), sem("lhi_done")
        llo_dve, llo_pool = sem("llo_dve"), sem("llo_pool")

        xh_in = [sem("xh_in0"), sem("xh_in1")]
        st1_done, mv1_done, rs1_done, xh_done = sem("st1_done"), sem("mv1_done"), sem("rs1_done"), sem("xh_done")
        hi_done, lo_done = sem("hi_done"), sem("lo_done")
        rs1_var = sem("rs1_var")
        x_in = [sem("x_in0"), sem("x_in1")]
        gn_mm, gT_done = sem("gn_mm"), sem("gT_done")
        w_mm, x1_done, st2_done, mv2_done = sem("w_mm"), sem("x1_done"), sem("st2_done"), sem("mv2_done")
        rs2_var, rs2_done, xn_done, xb_done = sem("rs2_var"), sem("rs2_done"), sem("xn_done"), sem("xb_done")
        t_mm, xnT_done = sem("t_mm"), sem("xnT_done")
        dt_mm, v_done, nab_done, e_done = sem("dt_mm"), sem("v_done"), sem("nab_done"), sem("e_done")
        chain, dA_done = sem("chain"), sem("dA_done")
        cum_mm, ncum_done = sem("cum_mm"), sem("ncum_done")
        split, parts_done, parts_mm, cumT_done = sem("split"), sem("parts_done"), sem("parts_mm"), sem("cumT_done")
        ip_mm, ip_free = sem("ip_mm"), sem("ip_free")
        tap, conv_done, silu_done = sem("tap"), sem("conv_done"), sem("silu_done")
        cc_in = sem("cc_in")
        g_mm, diff_mm, e_mm, mid_mm = sem("g_mm"), sem("diff_mm"), sem("e_mm"), sem("mid_mm")
        e_exp, l_exp = sem("e_exp"), sem("l_exp")
        dcy_done, dce_done, ce_done, xdd_done = sem("dcy_done"), sem("dce_done"), sem("ce_done"), sem("xdd_done")
        st_zero, xdt_done, m_done, yst_done = sem("st_zero"), sem("xdt_done"), sem("m_done"), sem("yst_done")
        gate_done, sq_done, sqs_done, ss_mm, ss_done = sem("gate_done"), sem("sq_done"), sem("sqs_done"), sem("ss_mm"), sem("ss_done")
        rms_done, out_mm, out_done = sem("rms_done"), sem("out_mm"), sem("out_done")
        stored = [sem("stored0"), sem("stored1")]

        def wait(eng, s, value):
            if isinstance(value, int) and value <= 0:
                return
            eng.wait_ge(s, value)

        def wait_apart(eng, s, value):
            wait(eng, s, value)
            if not isinstance(value, int):
                eng.sem_inc(unread, 1)

        def every_step(eng, step):
            for q in range(NQ):
                step(0, q, True, q >= 1, q >= 2, q >= 3)
            with eng.Fori(1, B - 1) as b:
                for q in range(NQ):
                    step(b, q, True, True, True, True)
            for q in range(NQ):
                step(B - 1, q, True, True, True, True)
            for q in range(3):
                step(B, q, False, q < 1, q < 2, True)

        sym_items = []
        for j in range(KT):
            for i0 in range(0, j, 4):
                n = min(4, j - i0)
                sym_items += [(j, i0, n, True), (j, i0, n, False)]
            sym_items.append((j, j, 1, True))
        sym_after = {j: max(m for m, it in enumerate(sym_items) if it[0] == j) + 1 for j in range(KT)}
        relu_items = sorted(((k, q) for k in range(KT) for q in range(NQ)), key=lambda it: max(it[0], 4 * it[1] + 3))
        relu_last = [it for it in relu_items if max(it[0], 4 * it[1] + 3) == KT - 1]
        relu_of_dve = relu_last[1::2]
        l_items = [(k, q) for q in range(NQ) for k in range(KT)]

        def on_pool(m):
            return m % 3 != 0

        def low_halves(m):
            return sum(not on_pool(i) for i in range(m)), sum(on_pool(i) for i in range(m))

        def fill(b, q, slot):
            if isinstance(b, int) and b == 0 and q == 0:
                return ((KT, 2 * KT), (2 * KT, 3 * KT))[slot] if slot < 2 else (0, 0)
            if isinstance(b, int) and b == 0 and q == 1:
                return 3 * KT + 4 * slot, 3 * KT + 4 * slot + 4
            return 0, 0

        def x_tiles(t, b, q):
            return t[b, q * GT:(q + 1) * GT, :].rearrange("(t p) f -> p t f", p=P)

        def b_and_q(b, q, back):
            return (b, q - back) if q >= back else (b - 1, q - back + NQ)

        def of_parity(b, q, back):
            return 2 * b + (q - back) // 2 + 1

        block = ctx.enter_context(nc.Block())

        @block.sync
        def _(sp):
            a_rows = adj.rearrange("(k p) n -> k p n", p=P)
            for k in range(KT):
                sp.dma_start(S_[:, k, :], a_rows[k]).then_inc(adj_in[k], 16)
                if k == 3:
                    small = [
                        (w_in[:, :], W_in), (w_gnn[:, :], gnn_W), (wl, W_lin),
                        (wo, W_out.rearrange("(j c) k -> c j k", c=P)),
                        (cw[:, :, :], conv_w.rearrange("(j c) k -> c j k", c=P)),
                        (cb_[:, :], conv_b.rearrange("(j c) -> c j", c=P)),
                        (nwc[:, :], norm_w.rearrange("(j c) -> c j", c=P)),
                        (dtb[:, :], dt_bias.partition_broadcast(P)),
                        (aexp[:, :], A_log.partition_broadcast(P)),
                        (blin[:, :], b_lin.partition_broadcast(P)),
                    ]
                    for hh in range(2):
                        small.append((dcol[hh * HD:(hh + 1) * HD, :],
                                      D.rearrange("(j h) -> h j", h=2)[hh].partition_broadcast(HD)))
                    for dst, src in small:
                        sp.dma_start(dst, src, allow_slow_non_contiguous=True).then_inc(w_landed, 16)
                if k in (2, 3, 6, 7):
                    q = (2, 3, 6, 7).index(k)
                    if q >= 2:
                        sp.wait_ge(xh_in[q % 2], 16)
                    sp.dma_start(xhat[:, q * GC:(q + 1) * GC, :], x_tiles(x, 0, q)).then_inc(xh_in[q % 2], 16)

            def step(b, q, gn, ap, bk, tl):
                s = b * NQ + q
                if gn:
                    wait(sp, stored[q % 2], 16 * of_parity(b, q, 4))
                    sp.dma_start(x1[:, q, :, :], x_tiles(x, b, q)).then_inc(x_in[q % 2], 16)
                    if not isinstance(b, int) or b < B - 1:
                        sp.wait_ge(lo_done, 4 * b + 4)
                        sp.wait_ge(hi_done, 4 * b + 4)
                        sp.dma_start(xhat[:, q * GC:(q + 1) * GC, :],
                                     x_tiles(x, b + 1, q)).then_inc(xh_in[q % 2], 16)
                if tl:
                    bt, qt = b_and_q(b, q, 3)
                    sp.wait_ge(out_done, s - 2)
                    sp.dma_start(x_tiles(out, bt, qt), x1[:, qt, :, :]).then_inc(stored[qt % 2], 16)
                if ap:
                    g, pr = s - 1, (q - 1) % 2
                    wait_apart(sp, silu_done, 5 * g + 1)
                    wait(sp, ce_done, 4 * g)
                    wait(sp, g_mm, 4 * g)
                    for hh in range(2):
                        sp.dma_start(CC[hh * DS:(hh + 1) * DS, :], xs[DS:2 * DS, pr, 2, :]).then_inc(cc_in, 16)

            every_step(sp, step)
            sp.wait_ge(stored[0], 16 * G_ALL // 2)
            sp.wait_ge(stored[1], 16 * G_ALL // 2)

        @block.gpsimd
        def _(pool):
            g_ = nc.gpsimd
            g_.memset(ident[:, :], 0.0)
            g_.memset(upper[:, :], 1.0)
            g_.memset(maskb[:, :], 0.0)
            g_.memset(pick[:, :, :], 0.0)
            g_.memset(half[:, :], -0.5)
            g_.memset(zero3[:, :], 0.0)
            g_.memset(onec[:, :], 1.0 / DI)
            g_.memset(ones, 1.0).then_inc(zeroed, 1)
            pool.wait_ge(zeroed, 1)
            g_.affine_select(out=ident[:, :], in_=ident[:, :], compare_op=ALU.not_equal, fill=1.0, base=0,
                             pattern=[[-1, P]], channel_multiplier=1).then_inc(zeroed, 1)
            g_.affine_select(out=upper[:, :], in_=upper[:, :], compare_op=ALU.is_ge, fill=0.0, base=0,
                             pattern=[[1, P]], channel_multiplier=-1)
            g_.affine_select(out=maskb[:, :], in_=maskb[:, :], compare_op=ALU.is_ge, fill=MASKED, base=0,
                             pattern=[[1, P]], channel_multiplier=-1)
            for part in range(3):
                g_.affine_select(out=pick[:, :, :], in_=pick[:, :, :], compare_op=ALU.not_equal, fill=-1.0,
                                 base=-16 * part, pattern=[[-1, 16], [0, HD]], channel_multiplier=1).then_inc(zeroed, 1)
                pool.wait_ge(zeroed, 3 + part)
            g_.tensor_copy(identb[:, :], ident[:, :])
            g_.memset(xdtb[:, :, :], 0.0)
            g_.memset(state[:, :, :, :], 0.0).then_inc(consts_pool, 1)

            def rstd1(n):
                wait_apart(pool, mv1_done, n + 1)
                wait_apart(pool, xh_done, n)
                g_.tensor_scalar(rs1[:, :], mv1[:, :, 1], EPS, None, ALU.add).then_inc(rs1_var, 1)
                pool.wait_ge(rs1_var, n + 1)
                g_.tensor_tensor(rs1[:, :], rs1[:, :], half[:, 0:GC], ALU.pow).then_inc(rs1_done, 1)

            for n in range(NQ):
                rstd1(n)

            pool.wait_ge(rsum_done, 1)
            g_.tensor_scalar(msk[:, :], rsum[:, :], 0.0, None, ALU.is_gt).then_inc(cinv_done, 1)
            g_.tensor_scalar(cinv[:, :], rsum[:, :], 1e-37, None, ALU.max).then_inc(cinv_done, 1)
            pool.wait_ge(cinv_done, 2)
            g_.tensor_tensor(cinv[:, :], cinv[:, :], half[:, :], ALU.pow).then_inc(cinv_done, 1)
            pool.wait_ge(cinv_done, 3)
            g_.tensor_tensor(cinv[:, :], cinv[:, :], msk[:, :], ALU.mult).then_inc(cinv_done, 1)
            pool.wait_ge(cinv_done, 4)
            g_.tensor_scalar(negc[:, :], cinv[:, :], -L_SCALE, None, ALU.mult).then_inc(cinv_done, 1)
            def lap_lo(m0, m1):
                for m in range(m0, m1):
                    if on_pool(m):
                        k, q = l_items[m]
                        pool.wait_ge(lhi_done, m + 1)
                        g_.tensor_tensor(L_[:, k, q, 1, :], ring[m % RING], L_[:, k, q, 0, :],
                                         ALU.subtract).then_inc(llo_pool, 1)

            lap_lo(0, KT)

            def chunk_decay_and_ce(h, c):
                cb = c % 2
                pool.wait_ge(e_exp, 4 * h + c + 1)
                wait_apart(pool, yst_done, 4 * h + c - 1)
                g_.tensor_copy(dce[:, cb, :], CE[:, cb, :, P - 1]).then_inc(dce_done, 1)
                if c == 0:
                    pool.wait_ge(cc_in, 32 * h + 32)
                pool.wait_ge(dce_done, 4 * h + c + 1)
                g_.tensor_tensor(CE[:, cb, :, :], CE[:, cb, :, :],
                                 over(CC[:, c * P:(c + 1) * P], 1, 2), ALU.mult).then_inc(ce_done, 1)

            def chunk_xdd(h, c):
                cb = c % 2
                pool.wait_ge(xdt_done, 4 * h + c + 1)
                pool.wait_ge(dcy_done, 4 * h + c + 1)
                wait(pool, mid_mm, 4 * h + c - 1)
                g_.tensor_tensor(xdd[:, cb, :, :, :].rearrange("p h j d -> p j h d"),
                                 xdtp[:, cb, :, 0:HD].rearrange("p (j h) d -> p j h d", h=2),
                                 over(dcy[:, cb, :].rearrange("p (j h) -> p j h", h=2), 3, HD),
                                 ALU.mult).then_inc(xdd_done, 1)

            def split_cum(g, pr):
                pool.wait_ge(ncum_done, g + 1)
                wait_apart(pool, parts_mm, g)
                nc_ = ncum[:, pr, :]
                g_.tensor_copy(parts[:, 0, :], nc_).then_inc(split, 1)
                pool.wait_ge(split, 3 * g + 1)
                g_.tensor_tensor(res[:, :], nc_, parts[:, 0, :], ALU.subtract).then_inc(split, 1)
                wait_apart(pool, split, 3 * g + 2)
                g_.tensor_copy(parts[:, 1, :], res[:, :]).then_inc(split, 1)
                pool.wait_ge(split, 3 * g + 3)
                g_.tensor_tensor(parts[:, 2, :], res[:, :], parts[:, 1, :], ALU.subtract).then_inc(parts_done, 1)

            def step(b, q, gn, ap, bk, tl):
                s = b * NQ + q
                g, h, t = s - 1, s - 2, s - 3
                pa, pb = (q - 1) % 2, q % 2
                last = isinstance(b, int) and b >= B - 1
                if gn and not ap:
                    lap_lo(*fill(b, q, 0))
                    lap_lo(*fill(b, q, 1))
                if bk:
                    chunk_decay_and_ce(h, 0)
                if tl:
                    pool.wait_ge(ss_done, t + 1)
                    wait(pool, out_done, t)
                    g_.tensor_tensor(rms[:, :], ssm[:, :], half[:, 0:GC], ALU.pow).then_inc(rms_done, 1)
                if ap:
                    wait_apart(pool, mv2_done, g + 1)
                    g_.tensor_scalar(rs2[:, :], mv2[:, :, 1], EPS, None, ALU.add).then_inc(rs2_var, 1)
                    pool.wait_ge(rs2_var, g + 1)
                    g_.tensor_tensor(rs2[:, :], rs2[:, :], half[:, 0:GC], ALU.pow).then_inc(rs2_done, 1)
                if bk:
                    chunk_xdd(h, 0)
                elif ap:
                    lap_lo(*fill(b, q, 0))
                if bk:
                    chunk_decay_and_ce(h, 1)
                    chunk_xdd(h, 1)
                if ap:
                    qa = (q - 1) % 4
                    pool.wait_ge(xn_done, g + 1)
                    g_.tensor_tensor(x1[:, qa, :, :], x1[:, qa, :, :], over(blin[:, :], 1, GC),
                                     ALU.add).then_inc(xb_done, 1)
                if ap and not bk:
                    lap_lo(*fill(b, q, 1))
                    lap_lo(*fill(b, q, 2))
                if gn and not last:
                    rstd1(s + NQ)
                if bk:
                    chunk_decay_and_ce(h, 2)
                    chunk_xdd(h, 2)
                if ap and not bk:
                    lap_lo(*fill(b, q, 3))
                if ap:
                    split_cum(g, pa)
                if bk:
                    chunk_decay_and_ce(h, 3)
                    chunk_xdd(h, 3)
                    pool.wait_ge(silu_done, 5 * h + 5)
                    pool.wait_ge(yst_done, 4 * h + 4)
                    g_.tensor_tensor(xs[:, pb, 0:2, :], xs[:, pb, 0:2, :], sz[:, pb, :, :],
                                     ALU.mult).then_inc(gate_done, 1)
                    pool.wait_ge(sq_done, h + 1)
                    g_.tensor_tensor(ysq[:, 0, :], ysq[:, 0, :], ysq[:, 1, :], ALU.add).then_inc(sqs_done, 1)

            every_step(pool, step)

        @block.scalar
        def _(act):
            a_ = nc.scalar
            act.wait_ge(w_landed, 16 * 12)
            a_.activation(aexp[:, :], aexp[:, :], ACT.Exp).then_inc(aexp_done, 1)

            def split_hi(kk, count):
                act.wait_ge(xh_done, count)
                a_.activation(lnx[:, 4 * kk:4 * kk + 4, 0, :], xhat[:, 4 * kk:4 * kk + 4, :],
                              ACT.Copy, scale=X_SCALE).then_inc(hi_done, 1)

            done = 0
            for k, q in relu_items:
                need = sym_after[max(k, 4 * q + 3)]
                if need > done:
                    if max(k, 4 * q + 3) in (9, 11, 13, 15):
                        kk = (max(k, 4 * q + 3) - 9) // 2
                        split_hi(kk, kk + 1)
                    if need == sym_after[KT - 1]:
                        act.wait_ge(wot_mm, 1)
                        a_.activation(woT, p_front[:, 0:2 * P].rearrange("p (j c) -> p j c", j=2),
                                      ACT.Copy).then_inc(wot_done, 1)
                    act.wait_ge(sym_add, need)
                    done = need
                if (k, q) not in relu_of_dve:
                    blk = S_[:, k, q * GT:(q + 1) * GT]
                    a_.activation(blk, blk, ACT.Relu, accum_out=rsp[:, k, q:q + 1]).then_inc(relu_act, 1)

            def lap_hi(m0, m1):
                for m in range(m0, m1):
                    k, q = l_items[m]
                    act.wait_ge(lt_done, m + 1)
                    if k // 4 == q:
                        act.wait_ge(ld_done, k + 1)
                    a_.activation(L_[:, k, q, 0, :], ring[m % RING], ACT.Copy).then_inc(lhi_done, 1)

            lap_hi(0, KT)

            def exps(h, c, pr):
                cb = c % 2
                wait(act, mid_mm, 4 * h + c - 1)
                act.wait_ge(e_mm, 4 * h + c + 1)
                a_.activation(CE[:, cb, :, :], p_e[:, 0:2 * P].rearrange("p (j l) -> p j l", j=2),
                              ACT.Exp).then_inc(e_exp, 1)
                act.wait_ge(diff_mm, 4 * h + c + 1)
                act.wait_ge(ncum_done, h + 1)
                for hh in range(H):
                    last = a_.activation(Lx[:, cb, hh, :], p_diff[:, hh * P:(hh + 1) * P], ACT.Exp,
                                         bias=ncum[:, pr, c * H + hh:c * H + hh + 1])
                last.then_inc(l_exp, 1)

            def conv_in(g, i, j, pr, first):
                n = 3 * g + i
                buf = (pr + i) % 2
                act.wait_ge(ip_mm, 5 * g + i + 1)
                wait(act, conv_done, n - 1)
                if i == 0:
                    wait(act, ss_mm, g - 1)
                    wait(act, out_mm, g - 1)
                wait(act, ip_free, 3 * (g - 1) + i + 1)
                a_.activation(xraw[:, buf, 0:3], zero3[:, 0:3] if first else halo[:, 1 - pr, j, :], ACT.Copy)
                a_.activation(xraw[:, buf, 3:3 + GT], p_ip[:, :], ACT.Copy)
                a_.activation(halo[:, pr, j, :], p_ip[:, GT - 3:GT], ACT.Copy)
                a_.activation(xs[:, pr, j, :], p_ip[:, :], ACT.Identity, bias=cb_[:, j:j + 1],
                              scale=cw[:, j, 3:4]).then_inc(ip_free, 1)

            def step(b, q, gn, ap, bk, tl):
                s = b * NQ + q
                g, h, t = s - 1, s - 2, s - 3
                pa, pb = (q - 1) % 2, q % 2
                last = isinstance(b, int) and b >= B - 1
                hi = gn and q == NQ - 1 and not last
                if gn and not ap:
                    lap_hi(*fill(b, q, 0))
                if gn and bk and not tl:
                    act.wait_ge(llo_dve, low_halves(len(l_items))[0])
                    act.wait_ge(llo_pool, low_halves(len(l_items))[1])
                if bk:
                    exps(h, 1, pb)
                elif ap:
                    lap_hi(*fill(b, q, 0))
                if ap:
                    act.wait_ge(t_mm, g + 1)
                    wait(act, ip_mm, 5 * g)
                    a_.activation(xnT[:, :], p_front[:, :], ACT.Copy).then_inc(xnT_done, 1)
                if bk:
                    exps(h, 2, pb)
                elif ap:
                    lap_hi(*fill(b, q, 1))
                if ap:
                    act.wait_ge(nab_done, g + 1)
                    a_.activation(e_dt[:, :], nab[:, :], ACT.Exp).then_inc(e_done, 1)
                    conv_in(g, 0, 2, pa, (q - 1) % 4 == 0)
                if hi:
                    act.wait_ge(gn_mm, 4 * s + 1)
                    split_hi(0, 4 * (b + 1) + 1)
                if ap and not bk:
                    lap_hi(*fill(b, q, 2))
                if ap:
                    conv_in(g, 1, 0, pa, (q - 1) % 4 == 0)
                if bk:
                    exps(h, 3, pb)
                elif ap:
                    lap_hi(*fill(b, q, 3))
                if ap:
                    act.wait_ge(cum_mm, g + 1)
                    a_.activation(ncum[:, pa, :], p_front[:, 32:48], ACT.Copy, scale=-1.0).then_inc(ncum_done, 1)
                    conv_in(g, 2, 1, pa, (q - 1) % 4 == 0)
                    act.wait_ge(parts_mm, g + 1)
                    a_.activation(cumT[:, pa, :], p_cumT, ACT.Copy).then_inc(cumT_done, 1)
                if hi:
                    act.wait_ge(gn_mm, 4 * s + 2)
                    split_hi(1, 4 * (b + 1) + 2)
                if ap:
                    for i, j in enumerate((2, 0, 1)):
                        act.wait_ge(conv_done, 3 * g + i + 1)
                        a_.activation(xs[:, pa, j, :], xs[:, pa, j, :], ACT.Silu).then_inc(silu_done, 1)
                    act.wait_ge(ip_mm, 5 * g + 4)
                    wait(act, gate_done, g - 1)
                    a_.activation(sz[:, pa, 0, :], p_ip[:, :], ACT.Silu).then_inc(silu_done, 1)
                if hi:
                    act.wait_ge(gn_mm, 4 * s + 3)
                    split_hi(2, 4 * (b + 1) + 3)
                if ap:
                    act.wait_ge(ip_mm, 5 * g + 5)
                    a_.activation(sz[:, pa, 1, :], p_ip[:, :], ACT.Silu).then_inc(silu_done, 1)
                if bk:
                    act.wait_ge(gate_done, h + 1)
                    wait(act, conv_done, 3 * (h + 2) if not isinstance(h, int) else 3 * min(h + 2, G_ALL))
                    a_.activation(ysq, xs[:, pb, 0:2, :], ACT.Square).then_inc(sq_done, 1)
                if gn:
                    act.wait_ge(gn_mm, 4 * s + 4)
                    wait(act, t_mm, s)
                    a_.activation(gT_xn[:, :], p_gn[:, :], ACT.Copy,
                                  scale=1.0 / (L_SCALE * X_SCALE)).then_inc(gT_done, 1)
                if gn and not ap:
                    lap_hi(*fill(b, q, 1))
                if hi:
                    split_hi(3, 4 * (b + 1) + 4)
                if ap:
                    exps(g, 0, pa)

            every_step(act, step)

        @block.vector
        def _(dve):
            v_ = nc.vector
            v_.memset(dce[:, :, :], 0.0)

            def norm1(n, q, cs=range(GC)):
                dve.wait_ge(rs1_done, n + 1)
                for c in cs:
                    xt = xhat[:, q * GC + c, :]
                    last = v_.tensor_scalar(xt, xt, mv1[:, c, 0:1], rs1[:, c:c + 1], ALU.subtract, ALU.mult)
                if c == GC - 1:
                    last.then_inc(xh_done, 1)

            def stats1(n, q, nth, cs=range(GC)):
                dve.wait_ge(xh_in[q % 2], 16 * nth)
                for c in cs:
                    last = v_.bn_stats(st1[:, c, :], xhat[:, q * GC + c, :])
                if c == GC - 1:
                    last.then_inc(st1_done, 1)

            def aggr1(n):
                dve.wait_ge(st1_done, n + 1)
                wait_apart(dve, xh_done, n)
                for c in range(GC):
                    last = v_.bn_aggr(mv1[:, c, :], st1[:, c, :])
                last.then_inc(mv1_done, 1)

            def split_lo(kk, count):
                dve.wait_ge(hi_done, count)
                v_.scalar_tensor_tensor(lnx[:, 4 * kk:4 * kk + 4, 1, :], xhat[:, 4 * kk:4 * kk + 4, :], X_SCALE,
                                        lnx[:, 4 * kk:4 * kk + 4, 0, :], ALU.mult, ALU.subtract).then_inc(lo_done, 1)

            for m, (j, i0, n, row) in enumerate(sym_items):
                dve.wait_ge(sym_mm, m + (2 if row and j != i0 else 1))
                dst = S_[:, j, i0 * P:(i0 + n) * P].rearrange("p (i n) -> p i n", i=n) if row \
                    else S_[:, i0:i0 + n, j * P:(j + 1) * P]
                v_.tensor_tensor(dst, dst, bank[m % 8][:, 0:n * P].rearrange("p (i n) -> p i n", i=n),
                                 ALU.add).then_inc(sym_add, 1)
                if m == 30:
                    dve.wait_ge(aexp_done, 1)
                    v_.tensor_scalar(aneg[:, :], aexp[:, :], -1.0, None, ALU.mult).then_inc(aneg_done, 1)
                if m + 1 == sym_after[j]:
                    if j in (7, 9, 11, 13):
                        stats1((j - 7) // 2, (j - 7) // 2, (j - 7) // 4 + 1)
                    if j in (11, 13, 15):
                        split_lo((j - 11) // 2, (j - 11) // 2 + 1)
                    if j in (7, 9, 11, 13):
                        aggr1((j - 7) // 2)
                    if j % 2 == 0 and j >= 8:
                        norm1((j - 8) // 2, (j - 8) // 2)


            dve.wait_ge(sym_add, len(sym_items))
            for k, q in relu_of_dve:
                blk = S_[:, k, q * GT:(q + 1) * GT]
                v_.scalar_tensor_tensor(blk, blk, 0.0, blk, ALU.max, ALU.max,
                                        accum_out=rsp[:, k, q:q + 1]).then_inc(relu_dve, 1)
            dve.wait_ge(relu_act, len(relu_items) - len(relu_of_dve))
            dve.wait_ge(relu_dve, len(relu_of_dve))
            v_.tensor_reduce(out=rsum[:, :], in_=rsp[:, :, :], axis=mybir.AxisListType.X,
                             op=ALU.add).then_inc(rsum_done, 1)
            split_lo(3, 4)
            dve.wait_ge(wc_mm, 1)
            for j in range(2):
                last = v_.tensor_scalar(wc[:, j, :], p_e[:, j * P:(j + 1) * P], nwc[:, j:j + 1], None, ALU.mult)
            last.then_inc(wc_done, 1)

            def diagonal(q):
                dve.wait_ge(cinv_done, 5)
                wait(dve, cbc_mm, q - 1)
                v_.tensor_tensor(diag[:, q % 2, :, :], over(ident[:, :], 1, GC), over(cinv[:, q * GC:(q + 1) * GC], 2, P),
                                 ALU.mult).then_inc(diag_done, 1)

            def lap_lo(m):
                if m >= 0 and not on_pool(m):
                    k, q = l_items[m]
                    dve.wait_ge(lhi_done, m + 1)
                    v_.tensor_tensor(L_[:, k, q, 1, :], ring[m % RING], L_[:, k, q, 0, :],
                                     ALU.subtract).then_inc(llo_dve, 1)

            def lap(m0, m1):
                for m in range(m0, m1):
                    k, q = l_items[m]
                    if m >= RING:
                        if on_pool(m - RING):
                            dve.wait_ge(llo_pool, low_halves(m - RING + 1)[1])
                        else:
                            dve.wait_ge(llo_dve, low_halves(m - RING + 1)[0])
                    if k == 0:
                        dve.wait_ge(cbc_mm, q + 1)
                    v_.scalar_tensor_tensor(ring[m % RING], S_[:, k, q * GT:(q + 1) * GT], negc[:, k:k + 1],
                                            p_col[q][:, :], ALU.mult, ALU.mult).then_inc(lt_done, 1)
                    if k // 4 == q:
                        dve.wait_ge(lt_done, m + 1)
                        dg = ring[m % RING][:, (k % 4) * P:(k % 4 + 1) * P]
                        v_.scalar_tensor_tensor(dg, ident[:, :], L_SCALE, dg, ALU.mult, ALU.add).then_inc(ld_done, 1)
                    if m - LAG not in drained:
                        lap_lo(m - LAG)

            drained = range(KT - LAG, KT)
            diagonal(0)
            diagonal(1)
            lap(0, 4)
            diagonal(2)
            lap(4, 8)
            diagonal(3)
            lap(8, KT)
            for m in drained:
                lap_lo(m)

            def pre(h, c, pr, first):
                cb = c % 2
                tg = p_tg[cb]
                if first and c == 0:
                    wait(dve, yst_done, 4 * h)
                    v_.memset(state[:, 0, :, :], 0.0)
                dve.wait_ge(g_mm, 4 * h + c + 1)
                wait(dve, mid_mm, 4 * h + c - 1)
                wait(dve, xdd_done, 4 * h + c - 1)
                dve.wait_ge(l_exp, 4 * h + c + 1)
                v_.tensor_copy(dcy[:, cb, :], Lx[:, cb, :, P - 1]).then_inc(dcy_done, 1)
                v_.tensor_tensor(xdtp[:, cb, :, 0:HD], tg[:, 0:DI].rearrange("p (h d) -> p h d", h=H),
                                 over(dtv[:, pr, c * H:(c + 1) * H], 2, HD), ALU.mult).then_inc(xdt_done, 1)
                v_.tensor_copy(Bp[:, cb, DS:2 * DS], tg[:, DI:DI + DS])
                dve.wait_ge(dcy_done, 4 * h + c + 1)
                v_.tensor_tensor(Lx[:, cb, :, :], over(tg[:, 320:448], 1, H), Lx[:, cb, :, :],
                                 ALU.mult).then_inc(m_done, 1)

            def post_state(h, c, js=range(2)):
                cb = c % 2
                dve.wait_ge(mid_mm, 4 * h + c + 1)
                for j in js:
                    for hh in range(2):
                        rows = slice(hh * DS, (hh + 1) * DS)
                        v_.scalar_tensor_tensor(
                            state[rows, 1 - cb, j, hh * HD:(hh + 1) * HD], state[rows, cb, j, hh * HD:(hh + 1) * HD],
                            dce[rows, cb, j:j + 1], p_y[rows, 2 * P + j * HD:2 * P + (j + 1) * HD], ALU.mult, ALU.add)

            def post_y(h, c, pr):
                for j in range(2):
                    xc = xs[:, pr, j, c * P:(c + 1) * P]
                    last = v_.scalar_tensor_tensor(xc, xc, dcol[:, j:j + 1], p_y[:, j * P:(j + 1) * P],
                                                   ALU.mult, ALU.add)
                last.then_inc(yst_done, 1)

            def link(g, n, pr):
                z, z2, poly = (ch[:, i, :] for i in range(3))
                if n == 0:
                    dve.wait_ge(e_done, g + 1)
                else:
                    wait_apart(dve, chain, DT_OPS * g + n)
                if n == 0:
                    ins = v_.tensor_scalar(z, e_dt[:, :], 2.0, None, ALU.add)
                elif n == 1:
                    ins = v_.reciprocal(z, z)
                elif n == 2:
                    ins = v_.tensor_tensor(z, e_dt[:, :], z, ALU.mult)
                elif n == 3:
                    ins = v_.tensor_tensor(z2, z, z, ALU.mult)
                elif n == 4:
                    ins = v_.tensor_scalar(poly, z2, ATANH[4], None, ALU.mult)
                elif n <= 7:
                    ins = v_.scalar_tensor_tensor(poly, poly, ATANH[8 - n], z2, ALU.add, ALU.mult)
                elif n == 8:
                    ins = v_.scalar_tensor_tensor(poly, poly, ATANH[0], z, ALU.add, ALU.mult)
                elif n == 9:
                    ins = v_.scalar_tensor_tensor(dtv[:, pr, :], v_dt[:, :], 0.0, poly, ALU.max, ALU.add)
                else:
                    ins = v_.tensor_tensor(dA[:, :].rearrange("p (c h) -> p c h", h=H),
                                           dtv[:, pr, :].rearrange("p (c h) -> p c h", h=H),
                                           over(aneg[:, :], 1, GC), ALU.mult)
                ins.then_inc(chain if n < DT_OPS else dA_done, 1)

            def conv_tap(g, i, j, k, pr):
                buf = (pr + i) % 2
                if k == 2:
                    dve.wait_ge(ip_free, 3 * g + i + 1)
                else:
                    dve.wait_ge(tap, 6 * g + 2 * i + 2 - k)
                acc = xs[:, pr, j, :]
                v_.scalar_tensor_tensor(acc, xraw[:, buf, k:k + GT], cw[:, j, k:k + 1], acc,
                                        ALU.mult, ALU.add).then_inc(tap if k else conv_done, 1)

            def step(b, q, gn, ap, bk, tl):
                s = b * NQ + q
                g, h, t = s - 1, s - 2, s - 3
                qa, qt = (q - 1) % 4, (q - 3) % 4
                pa, pb = (q - 1) % 2, q % 2
                first = (q - 2) % 4 == 0
                last = isinstance(b, int) and b >= B - 1
                ln1 = gn and not last
                nth = 2 * (b + 1) + q // 2 + 1
                if gn and not ap:
                    lap(*fill(b, q, 0))
                    lap(*fill(b, q, 1))
                if ap:
                    dve.wait_ge(w_mm, g + 1)
                    dve.wait_ge(x_in[pa], 16 * of_parity(b, q, 1))
                    xt = x1[:, qa, :, :]
                    v_.scalar_tensor_tensor(xt, p_front[:, :].rearrange("p (c f) -> p c f", c=GC), 0.0, xt,
                                            ALU.max, ALU.add).then_inc(x1_done, 1)
                if ap:
                    dve.wait_ge(x1_done, g + 1)
                    for c in range(GC):
                        ins = v_.bn_stats(st2[:, c, :], x1[:, qa, c, :])
                    ins.then_inc(st2_done, 1)
                if tl:
                    dve.wait_ge(ss_mm, t + 1)
                    wait(dve, rms_done, t)
                    v_.tensor_scalar(ssm[:, :], p_y[:, 384:384 + GC], EPS, None, ALU.add).then_inc(ss_done, 1)
                if ap:
                    wait_apart(dve, st2_done, g + 1)
                    for c in range(GC):
                        ins = v_.bn_aggr(mv2[:, c, :], st2[:, c, :])
                    ins.then_inc(mv2_done, 1)
                if bk:
                    pre(h, 0, pb, first)
                elif ap:
                    lap(*fill(b, q, 0))
                if ap:
                    dve.wait_ge(rs2_done, g + 1)
                    for c in range(GC):
                        ins = v_.tensor_scalar(gT_xn[:, c * P:(c + 1) * P], x1[:, qa, c, :], mv2[:, c, 0:1],
                                               rs2[:, c:c + 1], ALU.subtract, ALU.mult)
                    ins.then_inc(xn_done, 1)
                if tl:
                    dve.wait_ge(out_mm, t + 1)
                    dve.wait_ge(rms_done, t + 1)
                    dve.wait_ge(xb_done, t + 1)
                    for c in range(GC):
                        xt = x1[:, qt, c, :]
                        ins = v_.scalar_tensor_tensor(xt, p_ip[:, c * P:(c + 1) * P], rms[:, c:c + 1], xt,
                                                      ALU.mult, ALU.add)
                    ins.then_inc(out_done, 1)
                if bk:
                    pre(h, 1, pb, first)
                    post_state(h, 0)
                    post_y(h, 0, pb)
                elif ap:
                    lap(*fill(b, q, 1))
                if ap:
                    dve.wait_ge(dt_mm, g + 1)
                    wait(dve, dA_done, g)
                    v_.tensor_tensor(v_dt[:, :].rearrange("p (c h) -> p c h", h=H),
                                     p_front[:, 0:16].rearrange("p (c h) -> p c h", h=H),
                                     over(dtb[:, :], 1, GC), ALU.add).then_inc(v_done, 1)
                if ln1:
                    stats1(s + NQ, q, nth, [0])
                if ap:
                    dve.wait_ge(v_done, g + 1)
                    v_.scalar_tensor_tensor(nab[:, :], v_dt[:, :], -1.0, v_dt[:, :], ALU.mult, ALU.min).then_inc(nab_done, 1)
                if bk:
                    pre(h, 2, pb, first)
                elif ap:
                    lap(*fill(b, q, 2))
                if ap:
                    link(g, 0, pa)
                if ln1:
                    stats1(s + NQ, q, nth, [1])
                if ap:
                    link(g, 1, pa)
                if ln1:
                    stats1(s + NQ, q, nth, [2])
                if ap:
                    link(g, 2, pa)
                if ln1:
                    stats1(s + NQ, q, nth, [3])
                if ap:
                    link(g, 3, pa)
                if bk:
                    post_state(h, 1, [0])
                if ap:
                    link(g, 4, pa)
                if bk:
                    post_state(h, 1, [1])
                if ap:
                    link(g, 5, pa)
                if bk:
                    post_y(h, 1, pb)
                if ap:
                    link(g, 6, pa)
                if ln1:
                    aggr1(s + NQ)
                if ap:
                    link(g, 7, pa)
                    conv_tap(g, 0, 2, 2, pa)
                    link(g, 8, pa)
                    conv_tap(g, 0, 2, 1, pa)
                    link(g, 9, pa)
                    conv_tap(g, 0, 2, 0, pa)
                    link(g, 10, pa)
                    conv_tap(g, 1, 0, 2, pa)
                if bk:
                    pre(h, 3, pb, first)
                elif ap:
                    lap(*fill(b, q, 3))
                    for m in range(len(l_items) - LAG, len(l_items)):
                        lap_lo(m)
                if ap:
                    conv_tap(g, 1, 0, 1, pa)
                if bk:
                    post_state(h, 2)
                    post_y(h, 2, pb)
                if ap:
                    conv_tap(g, 1, 0, 0, pa)
                if ln1:
                    norm1(s + NQ, q, [0, 1])
                if ap:
                    conv_tap(g, 2, 1, 2, pa)
                if ln1:
                    norm1(s + NQ, q, [2])
                if ap:
                    conv_tap(g, 2, 1, 1, pa)
                if ln1:
                    norm1(s + NQ, q, [3])
                if ap:
                    conv_tap(g, 2, 1, 0, pa)
                if bk:
                    post_state(h, 3)
                    post_y(h, 3, pb)
                if ln1 and q == NQ - 1:
                    for kk in range(4):
                        split_lo(kk, 4 * (b + 1) + kk + 1)

            every_step(dve, step)

        @block.tensor
        def _(pe):
            t_ = nc.tensor
            pe.wait_ge(consts_pool, 1)
            for m, (j, i0, n, row) in enumerate(sym_items):
                if m == 0 or sym_items[m - 1][0] != j:
                    pe.wait_ge(adj_in[j], 16)
                if m >= 8:
                    pe.wait_ge(sym_add, m - 7)
                for i in range(n):
                    src = S_[:, i0 + i, j * P:(j + 1) * P] if row else S_[:, j, (i0 + i) * P:(i0 + i + 1) * P]
                    last = t_.transpose(bank[m % 8][:, i * P:(i + 1) * P], src, ident[:, :])
                last.then_inc(sym_mm, 1)
            pe.wait_ge(sym_add, len(sym_items))
            pe.wait_ge(w_landed, 16 * 12)
            for j in range(2):
                last = t_.transpose(p_front[:, j * P:(j + 1) * P], wo[:, j, :], ident[:, :])
            last.then_inc(wot_mm, 1)
            pe.wait_ge(wot_done, 1)
            for j in range(2):
                last = t_.matmul(p_e[:, j * P:(j + 1) * P], woT[:, j, :], wl, start=True, stop=True)
            last.then_inc(wc_mm, 1)
            pe.wait_ge(wc_done, 1)
            for q in range(NQ):
                pe.wait_ge(diag_done, q + 1)
                t_.matmul(p_col[q][:, :], ones, diag[:, q % 2, :, :].rearrange("p t n -> p (t n)"), start=True,
                          stop=True).then_inc(cbc_mm, 1)

            def laplacian(b, q, m0, m1):
                s = b * NQ + q
                for m in range(m0, m1):
                    k, term = m // 3, m % 3
                    if m == 0:
                        wait(pe, gT_done, s)
                        if isinstance(b, int) and b == 0:
                            pe.wait_ge(llo_dve, low_halves(KT * (q + 1))[0])
                            pe.wait_ge(llo_pool, low_halves(KT * (q + 1))[1])
                    if q == 0 and m % 12 == 0:
                        pe.wait_ge(lo_done, 4 * b + m // 12 + 1)
                        pe.wait_ge(hi_done, 4 * b + m // 12 + 1)
                    ins = t_.matmul(p_gn[:, :], lnx[:, k, term // 2, :], L_[:, k, q, term % 2, :],
                                    start=(m == 0), stop=(m == 3 * KT - 1))
                    if m % 12 == 11:
                        ins.then_inc(gn_mm, 1)

            def chunk_in(h, c, pr):
                cb = c % 2
                tg = p_tg[cb]
                cs = slice(c * P, (c + 1) * P)
                rows = cumT[:, pr, :]
                pe.wait_ge(cumT_done, h + 1)
                wait(pe, e_exp, 4 * h + c)
                for j in range(2):
                    ins = t_.matmul(p_e[:, j * P:(j + 1) * P], pick[:, c * H + 2 * j:c * H + 2 * j + 2, :].rearrange("r h d -> r (h d)"),
                                    rows, start=True, stop=True)
                ins.then_inc(e_mm, 1)
                wait(pe, l_exp, 4 * h + c)
                t_.matmul(p_diff[:, :], identb[:, :], over(maskb[:, :], 1, H), start=True, stop=False)
                for hh in range(H):
                    ins = t_.matmul(p_diff[:, hh * P:(hh + 1) * P], over(pick[:, c * H + hh, 0], 1, P), rows,
                                    start=False, stop=(hh == H - 1))
                ins.then_inc(diff_mm, 1)
                if c == 0:
                    pe.wait_ge(silu_done, 5 * h + 3)
                    pe.wait_ge(cc_in, 32 * h + 32)
                wait(pe, m_done, 4 * h + c - 1)
                t_.transpose(tg[:, 0:P], xs[:, pr, 0, cs], ident[:, :])
                t_.transpose(tg[:, P:2 * P], xs[:, pr, 1, cs], ident[:, :])
                t_.transpose(tg[:, DI:DI + DS], xs[0:DS, pr, 2, cs], ident[0:DS, 0:DS])
                t_.matmul(tg[:, 320:448], xs[0:DS, pr, 2, cs], CC[0:DS, cs], start=True, stop=True).then_inc(g_mm, 1)

            def chunk_out(h, c, tl):
                cb = c % 2
                pe.wait_ge(m_done, 4 * h + c + 1)
                pe.wait_ge(ce_done, 4 * h + c + 1)
                wait(pe, yst_done, 4 * h + c)
                if c == 0 and tl:
                    pe.wait_ge(ss_done, h)
                for j in range(2):
                    y = p_y[:, j * P:(j + 1) * P]
                    xp = xdtb[:, cb, :]
                    t_.matmul(y, xp[:, 4 * j * HD:4 * j * HD + P], Lx[:, cb, 2 * j, :], start=True, stop=False)
                    t_.matmul(y, xp[:, (4 * j + 1) * HD:(4 * j + 1) * HD + P], Lx[:, cb, 2 * j + 1, :],
                              start=False, stop=False)
                    t_.matmul(y, state[:, cb, j, :], CE[:, cb, j, :], start=False, stop=True)
                pe.wait_ge(xdd_done, 4 * h + c + 1)
                for hh in range(2):
                    ins = t_.matmul(p_y[:, 2 * P:3 * P], Bp[:, cb, (1 - hh) * DS:(1 - hh) * DS + P],
                                    xdd[:, cb, hh, :, :].rearrange("p j d -> p (j d)"), start=(hh == 0), stop=(hh == 1))
                ins.then_inc(mid_mm, 1)

            def project(g, i):
                col = (DI + 2 * P, DI, DI + P, 0, P)[i]
                if i in (1, 2, 3):
                    pe.wait_ge(ip_free, 3 * g + i)
                else:
                    wait(pe, silu_done, 5 * g + i)
                if i == 0:
                    wait(pe, out_done, g - 1)
                t_.matmul(p_ip[:, :], w_in[:, col:col + P], xnT[:, :], start=True, stop=True).then_inc(ip_mm, 1)

            def step(b, q, gn, ap, bk, tl):
                s = b * NQ + q
                g, h, t = s - 1, s - 2, s - 3
                pa, pb, pt = (q - 1) % 2, q % 2, (q - 3) % 2
                if ap:
                    pe.wait_ge(gT_done, g + 1)
                    wait(pe, cumT_done, g)
                    for c in range(GC):
                        ins = t_.matmul(p_front[:, c * P:(c + 1) * P], gT_xn[:, c * P:(c + 1) * P], w_gnn[:, :],
                                        start=True, stop=True)
                    ins.then_inc(w_mm, 1)
                if gn:
                    laplacian(b, q, 0, 4)
                if tl:
                    pe.wait_ge(sqs_done, t + 1)
                    pe.wait_ge(yst_done, 4 * t + 4)
                    for c in range(GC):
                        ins = t_.matmul(p_y[:, 384 + c:385 + c], ysq[:, 0, c * P:(c + 1) * P], onec[:, :],
                                        start=True, stop=True)
                    ins.then_inc(ss_mm, 1)
                    wait(pe, silu_done, 5 * (t + 2) if not isinstance(t, int) else 5 * min(t + 2, G_ALL))
                    for c in range(GC):
                        for j in range(2):
                            ins = t_.matmul(p_ip[:, c * P:(c + 1) * P], xs[:, pt, j, c * P:(c + 1) * P], wc[:, j, :],
                                            start=(j == 0), stop=(j == 1))
                    ins.then_inc(out_mm, 1)
                if bk:
                    chunk_in(h, 1, pb)
                    chunk_out(h, 0, tl)
                if gn:
                    laplacian(b, q, 4, 12)
                if ap:
                    pe.wait_ge(xn_done, g + 1)
                    for c in range(GC):
                        ins = t_.transpose(p_front[:, c * P:(c + 1) * P], gT_xn[:, c * P:(c + 1) * P], ident[:, :])
                    ins.then_inc(t_mm, 1)
                if bk:
                    chunk_in(h, 2, pb)
                if gn:
                    laplacian(b, q, 12, 15)
                if ap:
                    pe.wait_ge(xnT_done, g + 1)
                    for c in range(GC):
                        ins = t_.matmul(p_front[:, c * H:(c + 1) * H], xnT[:, c * P:(c + 1) * P],
                                        w_in[:, 2 * DI + 2 * DS:2 * DI + 2 * DS + H], start=True, stop=True)
                    ins.then_inc(dt_mm, 1)
                    project(g, 0)
                if gn:
                    laplacian(b, q, 15, 15)
                if bk:
                    chunk_out(h, 1, tl)
                if ap:
                    project(g, 1)
                if bk:
                    chunk_in(h, 3, pb)
                if gn:
                    laplacian(b, q, 15, 24)
                if ap:
                    pe.wait_ge(dA_done, g + 1)
                    t_.matmul(p_front[:, 32:48], upper[:, :], dA[:, :], start=True, stop=True).then_inc(cum_mm, 1)
                if bk:
                    chunk_out(h, 2, tl)
                if ap:
                    project(g, 2)
                if gn:
                    laplacian(b, q, 24, 31)
                if ap:
                    wait_apart(pe, parts_done, g + 1)
                    t_.transpose(p_cumT, parts[:, :, :].rearrange("p a b -> p (a b)"), identb[:, :]).then_inc(parts_mm, 1)
                if bk:
                    chunk_out(h, 3, tl)
                if ap:
                    project(g, 3)
                if gn:
                    laplacian(b, q, 31, 38)
                if ap:
                    project(g, 4)
                if gn:
                    laplacian(b, q, 38, 48)
                if ap and not bk:
                    pe.wait_ge(lt_done, len(l_items))
                if ap:
                    chunk_in(g, 0, pa)

            every_step(pe, step)


_INS = ["x", "adj", "L0_gnn_W", "L0_ffn_W_in", "L0_ffn_conv_w", "L0_ffn_conv_b", "L0_ffn_dt_bias", "L0_ffn_A_log",
        "L0_ffn_D", "L0_ffn_norm_w", "L0_ffn_W_out", "L0_ffn_W_lin", "L0_ffn_b_lin"]


def kernel(**inputs):
    import numpy as _np
    import concourse.bacc as _bacc
    from concourse import mybir as _mybir
    from concourse.bass_utils import run_bass_kernel_spmd as _run

    nc = _bacc.Bacc("TRN2", target_bir_lowering=False, num_devices=1)
    arrays, args = {}, []
    for name in _INS:
        a = _np.ascontiguousarray(inputs[name])
        arrays[f"in_{name}"] = a
        args.append(nc.dram_tensor(f"in_{name}", a.shape, _mybir.dt.from_np(a.dtype), kind="ExternalInput").ap())
    o = nc.dram_tensor("out", (B, N, F), F32, kind="ExternalOutput").ap()
    gnn_mamba(nc, *args, o)
    r = _run(nc, [arrays], core_ids=[0])
    return r.results[0]["out"]
```

```python
import concourse.bass as bass
from concourse import mybir
from contextlib import ExitStack

F32 = mybir.dt.float32
F16 = mybir.dt.float16
BF16 = mybir.dt.bfloat16
ACT = mybir.ActivationFunctionType
ALU = mybir.AluOpType

P = 128
B, N, F = 8, 2048, 128
KT = N // P
GC = 4
GT = GC * P
NQ = N // GT
G_ALL = B * NQ
H, HD, DS = 4, 64, 64
DI = H * HD
TAPS = 4
EPS = 1e-5
L_SCALE = 4096.0
X_SCALE = 1024.0
ATANH = [2.0000000078777487, 0.6666631593508168, 0.4002485372344133, 0.2796141883517147, 0.2817465726146668]
DT_OPS = 10


def over(ap, axis, n):
    a = ap.unsqueeze(axis)
    shape = list(a.shape)
    shape[axis] = n
    return a.to_broadcast(shape)


def gnn_mamba(nc, x, adj, gnn_W, W_in, conv_w, conv_b, dt_bias, A_log, D, norm_w, W_out, W_lin, b_lin, out):
    with ExitStack() as ctx:
        def sb(name, shape, dt=F32):
            return ctx.enter_context(nc.sbuf_tensor(name, shape, dt))

        def sem(name):
            return ctx.enter_context(nc.semaphore(name))

        lap = sb("lap", [P, KT * N])
        S_ = lap[:, :].rearrange("p (k n) -> p k n", k=KT)
        L_ = lap[:, :].bitcast(F16).rearrange("p (k q t n) -> p k q t n", k=KT, q=NQ, t=2)
        lnx = sb("lnx", [P, KT, 2, F], F16)
        xhat = sb("xhat", [P, KT, F])
        gT_xn = sb("gT_xn", [P, GT])
        x1 = sb("x1", [P, NQ, GC, F])
        xnT = sb("xnT", [P, GT])
        xraw = sb("xraw", [P, 2, TAPS - 1 + GT])
        ysq = xraw[:, :, :].rearrange("p a b -> p (a b)")[:, 0:2 * GT].rearrange("p (j t) -> p j t", j=2)
        halo = sb("halo", [P, 2, 3, TAPS - 1])
        xs = sb("xs", [P, 2, 3, GT])
        sz = sb("sz", [P, 2, 2, GT])
        CC = sb("CC", [P, GT])
        Lx = sb("Lx", [P, 2, H, P])
        CE = sb("CE", [P, 2, 2, P])
        xdtb = sb("xdtb", [P, 2, 2 * H * HD + 2 * DS])
        xdtp = xdtb[:, :, 0:2 * H * HD].rearrange("p a (h d) -> p a h d", h=H)
        Bp = xdtb[:, :, (2 * H - 1) * HD:]
        xdd = sb("xdd", [P, 2, 2, 2, HD])
        state = sb("state", [P, 2, 2, P])
        w_in = sb("w_in", [P, 2 * DI + 2 * DS + H])
        w_gnn = sb("w_gnn", [P, F])
        wc = sb("wc", [P, 2, F])
        ident = sb("ident", [P, P])
        upper = sb("upper", [P, P])
        onec = sb("onec", [P, 1])
        identb = sb("identb", [P, P], BF16)
        Gm = sb("Gm", [P, P])
        pick = sb("pick", [48, 16, HD], BF16)
        zero3 = sb("zero3", [P, 4])
        cw = sb("cw", [P, 3, TAPS])
        cb_ = sb("cb_", [P, 3])
        dcol = sb("dcol", [P, 2])
        nwc = sb("nwc", [P, 2])
        dtb = sb("dtb", [P, H])
        aexp = sb("aexp", [P, H])
        aneg = sb("aneg", [P, H])
        blin = sb("blin", [P, F])
        half = sb("half", [P, 16])
        negc = sb("negc", [P, KT])
        st1 = sb("st1", [P, GC, 6])
        mv1 = sb("mv1", [P, GC, 2])
        rs1 = sb("rs1", [P, GC])
        st2 = sb("st2", [P, GC, 6])
        mv2 = sb("mv2", [P, GC, 2])
        rs2 = sb("rs2", [P, GC])
        v_dt = sb("v_dt", [P, 16])
        nab = sb("nab", [P, 16])
        e_dt = sb("e_dt", [P, 16])
        ch = sb("ch", [P, 5, 16])
        dtv = sb("dtv", [P, 2, 16])
        dA = sb("dA", [P, 16])
        cum = sb("cum", [P, 2, 16])
        res = sb("res", [P, 16])
        parts = sb("parts", [P, 3, 16], BF16)
        cumT = sb("cumT", [48, 2, P], BF16)
        dcy = sb("dcy", [P, 2, H])
        dce = sb("dce", [P, 2, 2])
        ssm = sb("ssm", [P, GC])
        rms = sb("rms", [P, GC])

        diag = sz[:, 0, :, :].rearrange("p a (t n) -> p a t n", t=GC)
        ring = [xs[:, 1, 0, :], xs[:, 1, 1, :], xs[:, 1, 2, :], sz[:, 1, 0, :], sz[:, 1, 1, :],
                Lx[:, 1, :, :].rearrange("p h l -> p (h l)")]
        RING = len(ring)
        LAG = 3
        ones = xs[:, 0, 0, 0:P]
        rsp = xnT[:, 0:KT * (NQ + 1)].rearrange("p (k q) -> p k q", k=KT)
        rsum, cinv, msk = (xnT[:, KT * (NQ + 1 + i):KT * (NQ + 2 + i)] for i in range(3))
        wo = Lx[:, 0, 0:2, :]
        woT = Lx[:, 1, 0:2, :]
        wl = Lx[:, 0, 2, :]

        bank = [ctx.enter_context(nc.psum_tensor(f"bank{i}", [P, 512], F32)) for i in range(8)]
        p_gn, p_front, p_ip, p_diff, p_e, p_y = bank[0], bank[1], bank[2], bank[3], bank[4], bank[5]
        p_tg = [bank[6], bank[7]]
        p_col = [p_e, p_y, p_tg[0], p_tg[1]]
        p_cumT = p_front[0:48, 64:128].bitcast(BF16)

        adj_in = [sem(f"adj_in{i}") for i in range(KT)]
        w_landed = sem("w_landed")
        consts_pool = sem("consts_pool")
        zeroed = sem("zeroed")
        unread = sem("unread")
        aexp_done, aneg_done = sem("aexp_done"), sem("aneg_done")
        wot_mm, wot_done, wc_mm, wc_done = sem("wot_mm"), sem("wot_done"), sem("wc_mm"), sem("wc_done")
        sym_mm, sym_add = sem("sym_mm"), sem("sym_add")
        relu_act, relu_dve, rsum_done, cinv_done = sem("relu_act"), sem("relu_dve"), sem("rsum_done"), sem("cinv_done")
        diag_done, cbc_mm = sem("diag_done"), sem("cbc_mm")
        lt_done, ld_done, lhi_done = sem("lt_done"), sem("ld_done"), sem("lhi_done")
        llo_dve, llo_pool = sem("llo_dve"), sem("llo_pool")

        xh_in = [sem("xh_in0"), sem("xh_in1")]
        st1_done, mv1_done, rs1_done, xh_done = sem("st1_done"), sem("mv1_done"), sem("rs1_done"), sem("xh_done")
        hi_done, lo_done = sem("hi_done"), sem("lo_done")
        rs1_var = sem("rs1_var")
        x_in = [sem("x_in0"), sem("x_in1")]
        gn_mm, gT_done = sem("gn_mm"), sem("gT_done")
        w_mm, x1_done, st2_done, mv2_done = sem("w_mm"), sem("x1_done"), sem("st2_done"), sem("mv2_done")
        rs2_var, rs2_done, xn_done, xb_done = sem("rs2_var"), sem("rs2_done"), sem("xn_done"), sem("xb_done")
        t_mm, xnT_done = sem("t_mm"), sem("xnT_done")
        dt_mm, v_done, nab_done, e_done = sem("dt_mm"), sem("v_done"), sem("nab_done"), sem("e_done")
        chain, dA_done = sem("chain"), sem("dA_done")
        cum_mm, cum_done = sem("cum_mm"), sem("cum_done")
        split, parts_done, parts_mm, cumT_done = sem("split"), sem("parts_done"), sem("parts_mm"), sem("cumT_done")
        ip_mm, ip_free = sem("ip_mm"), sem("ip_free")
        raw_done, tap3_done, tap = sem("raw_done"), sem("tap3_done"), sem("tap")
        conv_done, silu_done = sem("conv_done"), sem("silu_done")
        cc_in = sem("cc_in")
        g_mm, diff_mm, e_mm, mid_mm = sem("g_mm"), sem("diff_mm"), sem("e_mm"), sem("mid_mm")
        e_exp, drop_done, l_exp, gm_done = sem("e_exp"), sem("drop_done"), sem("l_exp"), sem("gm_done")
        dcy_done, dce_done, ce_done, xdd_done = sem("dcy_done"), sem("dce_done"), sem("ce_done"), sem("xdd_done")
        xdt_done, m_done, yst_done = sem("xdt_done"), sem("m_done"), sem("yst_done")
        gate_done, sq_done, sqs_done, ss_mm, ss_done = sem("gate_done"), sem("sq_done"), sem("sqs_done"), sem("ss_mm"), sem("ss_done")
        rms_done, out_mm, out_done = sem("rms_done"), sem("out_mm"), sem("out_done")
        stored = [sem("stored0"), sem("stored1")]

        def wait(eng, s, value):
            if isinstance(value, int) and value <= 0:
                return
            eng.wait_ge(s, value)

        def wait_apart(eng, s, value):
            wait(eng, s, value)
            if not isinstance(value, int):
                eng.sem_inc(unread, 1)

        def every_step(eng, step):
            for q in range(NQ):
                step(0, q, True, q >= 1, q >= 2, q >= 3)
            with eng.Fori(1, B - 1) as b:
                for q in range(NQ):
                    step(b, q, True, True, True, True)
            for q in range(NQ):
                step(B - 1, q, True, True, True, True)
            for q in range(3):
                step(B, q, False, q < 1, q < 2, True)

        bank_items, mirrors = [], []
        for j in range(KT):
            groups = [(i0, min(4, j - i0)) for i0 in range(0, j, 4)]
            bank_items += [("sum", j, i0, n) for i0, n in groups] + [("sum", j, j, 1)] + mirrors
            mirrors = [("mirror", j, i0, n) for i0, n in groups]
        bank_items += mirrors
        uppers = {j: [(k, j // 4) for k in range(j + 1)] if j % 4 == 3 else [] for j in range(KT)}
        n_sums = sum(it[0] == "sum" for it in bank_items)
        n_relus = len(bank_items) - n_sums + sum(len(u) for u in uppers.values())

        def dve_upper(k, q):
            return q >= 2 and (k % 2 == 1 or k in (0, 6) and q == 3)

        def items_to(kind, m):
            return sum(it[0] == kind for it in bank_items[:m])

        def strip_end(j):
            return 1 + max(m for m, it in enumerate(bank_items) if it[1] == j)

        def relus_before(m):
            ends = [u for j in range(KT) if strip_end(j) <= m and j < KT - 1 for u in uppers[j]]
            return items_to("mirror", m) + sum(not dve_upper(k, q) for k, q in ends)

        def sum_index(j, i0):
            return items_to("sum", bank_items.index(("sum", j, i0, min(4, j - i0))))

        def upper_row(k, q):
            return S_[:, k, max(k, 4 * q) * P:(q + 1) * GT]

        l_items = [(k, q) for q in range(NQ) for k in range(KT)]

        def on_pool(m):
            return m % 3 != 0 if m < KT else m % 6 != 0

        def low_halves(m):
            return sum(not on_pool(i) for i in range(m)), sum(on_pool(i) for i in range(m))

        def fill(b, q, slot):
            if isinstance(b, int) and b == 0 and q == 0:
                return (KT, 2 * KT) if slot == 0 else (0, 0)
            if isinstance(b, int) and b == 0 and q == 1:
                return 2 * KT + 8 * slot, 2 * KT + 8 * slot + 8
            return 0, 0

        def x_tiles(t, b, q):
            return t[b, q * GT:(q + 1) * GT, :].rearrange("(t p) f -> p t f", p=P)

        def b_and_q(b, q, back):
            return (b, q - back) if q >= back else (b - 1, q - back + NQ)

        def of_parity(b, q, back):
            return 2 * b + (q - back) // 2 + 1

        block = ctx.enter_context(nc.Block())

        @block.sync
        def _(sp):
            a_rows = adj.rearrange("(k p) n -> k p n", p=P)
            for k in range(KT):
                sp.dma_start(S_[:, k, :], a_rows[k]).then_inc(adj_in[k], 16)
                if k == 3:
                    small = [
                        (w_in[:, :], W_in), (w_gnn[:, :], gnn_W), (wl, W_lin),
                        (wo, W_out.rearrange("(j c) k -> c j k", c=P)),
                        (cw[:, :, :], conv_w.rearrange("(j c) k -> c j k", c=P)),
                        (cb_[:, :], conv_b.rearrange("(j c) -> c j", c=P)),
                        (nwc[:, :], norm_w.rearrange("(j c) -> c j", c=P)),
                        (dtb[:, :], dt_bias.partition_broadcast(P)),
                        (aexp[:, :], A_log.partition_broadcast(P)),
                        (blin[:, :], b_lin.partition_broadcast(P)),
                    ]
                    for hh in range(2):
                        small.append((dcol[hh * HD:(hh + 1) * HD, :],
                                      D.rearrange("(j h) -> h j", h=2)[hh].partition_broadcast(HD)))
                    for dst, src in small:
                        sp.dma_start(dst, src, allow_slow_non_contiguous=True).then_inc(w_landed, 16)
                if k in (1, 2, 5, 6):
                    q = (1, 2, 5, 6).index(k)
                    if q >= 2:
                        sp.wait_ge(xh_in[q % 2], 16)
                    sp.dma_start(xhat[:, q * GC:(q + 1) * GC, :], x_tiles(x, 0, q)).then_inc(xh_in[q % 2], 16)

            def step(b, q, gn, ap, bk, tl):
                s = b * NQ + q
                if gn:
                    wait(sp, stored[q % 2], 16 * of_parity(b, q, 4))
                    sp.dma_start(x1[:, q, :, :], x_tiles(x, b, q)).then_inc(x_in[q % 2], 16)
                    if not isinstance(b, int) or b < B - 1:
                        sp.wait_ge(lo_done, 4 * b + 4)
                        sp.wait_ge(hi_done, 4 * b + 4)
                        sp.dma_start(xhat[:, q * GC:(q + 1) * GC, :],
                                     x_tiles(x, b + 1, q)).then_inc(xh_in[q % 2], 16)
                if tl:
                    bt, qt = b_and_q(b, q, 3)
                    sp.wait_ge(out_done, s - 2)
                    sp.dma_start(x_tiles(out, bt, qt), x1[:, qt, :, :]).then_inc(stored[qt % 2], 16)
                if ap:
                    g, pr = s - 1, (q - 1) % 2
                    wait_apart(sp, silu_done, 5 * g + 1)
                    wait(sp, ce_done, 4 * g)
                    wait(sp, g_mm, 4 * g)
                    for hh in range(2):
                        sp.dma_start(CC[hh * DS:(hh + 1) * DS, :], xs[DS:2 * DS, pr, 2, :]).then_inc(cc_in, 16)

            every_step(sp, step)
            sp.wait_ge(stored[0], 16 * G_ALL // 2)
            sp.wait_ge(stored[1], 16 * G_ALL // 2)

        @block.gpsimd
        def _(pool):
            g_ = nc.gpsimd
            g_.memset(ident[:, :], 0.0)
            g_.memset(upper[:, :], 1.0)
            g_.memset(pick[:, :, :], 0.0)
            g_.memset(half[:, :], -0.5)
            g_.memset(zero3[:, :], 0.0)
            g_.memset(onec[:, :], 1.0 / DI)
            g_.memset(ones, 1.0).then_inc(zeroed, 1)
            pool.wait_ge(zeroed, 1)
            g_.affine_select(out=ident[:, :], in_=ident[:, :], compare_op=ALU.not_equal, fill=1.0, base=0,
                             pattern=[[-1, P]], channel_multiplier=1).then_inc(zeroed, 1)
            g_.affine_select(out=upper[:, :], in_=upper[:, :], compare_op=ALU.is_ge, fill=0.0, base=0,
                             pattern=[[1, P]], channel_multiplier=-1)
            for part in range(3):
                g_.affine_select(out=pick[:, :, :], in_=pick[:, :, :], compare_op=ALU.not_equal, fill=-1.0,
                                 base=-16 * part, pattern=[[-1, 16], [0, HD]], channel_multiplier=1).then_inc(zeroed, 1)
                pool.wait_ge(zeroed, 3 + part)
            g_.tensor_copy(identb[:, :], ident[:, :])
            g_.memset(xdtb[:, :, :], 0.0)
            g_.memset(state[:, :, :, :], 0.0).then_inc(consts_pool, 1)

            def rstd1(n):
                wait_apart(pool, mv1_done, n + 1)
                wait_apart(pool, xh_done, n)
                g_.tensor_scalar(rs1[:, :], mv1[:, :, 1], EPS, None, ALU.add).then_inc(rs1_var, 1)
                pool.wait_ge(rs1_var, n + 1)
                g_.tensor_tensor(rs1[:, :], rs1[:, :], half[:, 0:GC], ALU.pow).then_inc(rs1_done, 1)

            def norm1(n, q):
                wait_apart(pool, rs1_done, n + 1)
                for c in range(GC):
                    xt = xhat[:, q * GC + c, :]
                    last = g_.tensor_scalar(xt, xt, mv1[:, c, 0:1], rs1[:, c:c + 1], ALU.subtract, ALU.mult)
                last.then_inc(xh_done, 1)

            for n in range(NQ):
                rstd1(n)
                norm1(n, n)

            pool.wait_ge(rsum_done, 1)
            g_.tensor_scalar(msk[:, :], rsum[:, :], 0.0, None, ALU.is_gt).then_inc(cinv_done, 1)
            g_.tensor_scalar(cinv[:, :], rsum[:, :], 1e-37, None, ALU.max).then_inc(cinv_done, 1)
            pool.wait_ge(cinv_done, 2)
            g_.tensor_tensor(cinv[:, :], cinv[:, :], half[:, :], ALU.pow).then_inc(cinv_done, 1)
            pool.wait_ge(cinv_done, 3)
            g_.tensor_tensor(cinv[:, :], cinv[:, :], msk[:, :], ALU.mult).then_inc(cinv_done, 1)
            pool.wait_ge(cinv_done, 4)
            g_.tensor_scalar(negc[:, :], cinv[:, :], -L_SCALE, None, ALU.mult).then_inc(cinv_done, 1)
            def lap_lo(m0, m1):
                for m in range(m0, m1):
                    if on_pool(m):
                        k, q = l_items[m]
                        pool.wait_ge(lhi_done, m + 1)
                        g_.tensor_tensor(L_[:, k, q, 1, :], ring[m % RING], L_[:, k, q, 0, :],
                                         ALU.subtract).then_inc(llo_pool, 1)

            lap_lo(0, KT)

            def chunk_decay_and_ce(h, c):
                cb = c % 2
                pool.wait_ge(e_exp, 4 * h + c + 1)
                wait_apart(pool, yst_done, 4 * h + c - 1)
                g_.tensor_copy(dce[:, cb, :], CE[:, cb, :, P - 1]).then_inc(dce_done, 1)
                if c == 0:
                    pool.wait_ge(cc_in, 32 * h + 32)
                pool.wait_ge(dce_done, 4 * h + c + 1)
                g_.tensor_tensor(CE[:, cb, :, :], CE[:, cb, :, :],
                                 over(CC[:, c * P:(c + 1) * P], 1, 2), ALU.mult).then_inc(ce_done, 1)

            def chunk_xdd(h, c):
                cb = c % 2
                pool.wait_ge(xdt_done, 4 * h + c + 1)
                pool.wait_ge(dcy_done, 4 * h + c + 1)
                wait(pool, mid_mm, 4 * h + c - 1)
                g_.tensor_tensor(xdd[:, cb, :, :, :].rearrange("p h j d -> p j h d"),
                                 xdtp[:, cb, :, 0:HD].rearrange("p (j h) d -> p j h d", h=2),
                                 over(dcy[:, cb, :].rearrange("p (j h) -> p j h", h=2), 3, HD),
                                 ALU.mult).then_inc(xdd_done, 1)

            def split_cum(g, pr):
                pool.wait_ge(cum_done, g + 1)
                wait_apart(pool, parts_mm, g)
                cum_g = cum[:, pr, :]
                g_.tensor_copy(parts[:, 0, :], cum_g).then_inc(split, 1)
                pool.wait_ge(split, 3 * g + 1)
                g_.tensor_tensor(res[:, :], cum_g, parts[:, 0, :], ALU.subtract).then_inc(split, 1)
                wait_apart(pool, split, 3 * g + 2)
                g_.tensor_copy(parts[:, 1, :], res[:, :]).then_inc(split, 1)
                pool.wait_ge(split, 3 * g + 3)
                g_.tensor_tensor(parts[:, 2, :], res[:, :], parts[:, 1, :], ALU.subtract).then_inc(parts_done, 1)

            def step(b, q, gn, ap, bk, tl):
                s = b * NQ + q
                g, h, t = s - 1, s - 2, s - 3
                pa, pb = (q - 1) % 2, q % 2
                last = isinstance(b, int) and b >= B - 1
                if gn and not ap:
                    lap_lo(*fill(b, q, 0))
                    lap_lo(*fill(b, q, 1))
                if bk:
                    chunk_decay_and_ce(h, 0)
                if tl:
                    pool.wait_ge(ss_done, t + 1)
                    wait(pool, out_done, t)
                    g_.tensor_tensor(rms[:, :], ssm[:, :], half[:, 0:GC], ALU.pow).then_inc(rms_done, 1)
                if ap:
                    wait_apart(pool, mv2_done, g + 1)
                    g_.tensor_scalar(rs2[:, :], mv2[:, :, 1], EPS, None, ALU.add).then_inc(rs2_var, 1)
                    pool.wait_ge(rs2_var, g + 1)
                    g_.tensor_tensor(rs2[:, :], rs2[:, :], half[:, 0:GC], ALU.pow).then_inc(rs2_done, 1)
                if bk:
                    chunk_xdd(h, 0)
                elif ap:
                    lap_lo(*fill(b, q, 0))
                if bk:
                    chunk_decay_and_ce(h, 1)
                    chunk_xdd(h, 1)
                if ap:
                    qa = (q - 1) % 4
                    pool.wait_ge(xn_done, g + 1)
                    g_.tensor_tensor(x1[:, qa, :, :], x1[:, qa, :, :], over(blin[:, :], 1, GC),
                                     ALU.add).then_inc(xb_done, 1)
                if ap and not bk:
                    lap_lo(*fill(b, q, 1))
                    lap_lo(*fill(b, q, 2))
                if gn and not last:
                    rstd1(s + NQ)
                if bk:
                    chunk_decay_and_ce(h, 2)
                    chunk_xdd(h, 2)
                if ap and not bk:
                    lap_lo(*fill(b, q, 3))
                if ap:
                    split_cum(g, pa)
                if bk:
                    chunk_decay_and_ce(h, 3)
                    chunk_xdd(h, 3)
                if gn and not last:
                    norm1(s + NQ, q)
                if bk:
                    pool.wait_ge(sq_done, h + 1)
                    g_.tensor_tensor(ysq[:, 0, :], ysq[:, 0, :], ysq[:, 1, :], ALU.add).then_inc(sqs_done, 1)

            every_step(pool, step)

        @block.scalar
        def _(act):
            a_ = nc.scalar
            act.wait_ge(w_landed, 16 * 12)
            a_.activation(aexp[:, :], aexp[:, :], ACT.Exp).then_inc(aexp_done, 1)

            def split_hi(kk, count):
                act.wait_ge(xh_done, count)
                a_.activation(lnx[:, 4 * kk:4 * kk + 4, 0, :], xhat[:, 4 * kk:4 * kk + 4, :],
                              ACT.Copy, scale=X_SCALE).then_inc(hi_done, 1)

            for m, (kind, j, i0, n) in enumerate(bank_items):
                if kind == "mirror":
                    act.wait_ge(sym_mm, m + 1)
                    a_.activation(S_[:, j, i0 * P:(i0 + n) * P], bank[m % 8][:, 0:n * P], ACT.Relu,
                                  accum_out=rsp[:, j, (i0 // 4 if n == 4 else NQ):(i0 // 4 if n == 4 else NQ) + 1]
                                  ).then_inc(relu_act, 1)
                if m + 1 == strip_end(j):
                    if j in (6, 8, 10, 12):
                        split_hi((j - 6) // 2, (j - 6) // 2 + 1)
                    if j == KT - 1:
                        act.wait_ge(wot_mm, 1)
                        a_.activation(woT, p_front[:, 0:2 * P].rearrange("p (j c) -> p j c", j=2),
                                      ACT.Copy).then_inc(wot_done, 1)
                    act.wait_ge(sym_add, items_to("sum", m + 1))
                    act.wait_ge(sym_mm, m + 1)
                    for k, q in uppers[j]:
                        if not dve_upper(k, q):
                            a_.activation(upper_row(k, q), upper_row(k, q), ACT.Relu,
                                          accum_out=rsp[:, k, q:q + 1]).then_inc(relu_act, 1)

            def lap_hi(m0, m1):
                for m in range(m0, m1):
                    k, q = l_items[m]
                    act.wait_ge(lt_done, m + 1)
                    if k // 4 == q:
                        act.wait_ge(ld_done, k + 1)
                    a_.activation(L_[:, k, q, 0, :], ring[m % RING], ACT.Copy).then_inc(lhi_done, 1)

            lap_hi(0, KT)

            def exps(h, c, pr):
                cb = c % 2
                wait(act, mid_mm, 4 * h + c - 1)
                act.wait_ge(e_mm, 4 * h + c + 1)
                act.wait_ge(diff_mm, 4 * h + c + 1)
                act.wait_ge(cum_done, h + 1)
                for hh in range(H):
                    last = a_.activation(Lx[:, cb, hh, :], p_diff[:, hh * P:(hh + 1) * P], ACT.Relu,
                                         bias=cum[:, pr, c * H + hh:c * H + hh + 1])
                last.then_inc(drop_done, 1)
                a_.activation(CE[:, cb, :, :], p_e[:, 0:2 * P].rearrange("p (j l) -> p j l", j=2),
                              ACT.Exp, scale=-1.0).then_inc(e_exp, 1)
                act.wait_ge(drop_done, 4 * h + c + 1)
                a_.activation(Lx[:, cb, :, :], Lx[:, cb, :, :], ACT.Exp, scale=-1.0).then_inc(l_exp, 1)

            def conv_in(g, i, j, pr, first):
                n = 3 * g + i
                buf = (pr + i) % 2
                wait(act, conv_done, n - 1)
                if i == 0:
                    wait(act, ss_mm, g - 1)
                    wait(act, out_mm, g - 1)
                wait(act, ip_free, 3 * (g - 1) + i + 1)
                a_.activation(xraw[:, buf, 0:3], zero3[:, 0:3] if first else halo[:, 1 - pr, j, :], ACT.Copy)
                act.wait_ge(ip_mm, 5 * g + i + 1)
                a_.activation(xraw[:, buf, 3:3 + GT], p_ip[:, :], ACT.Copy).then_inc(raw_done, 1)
                a_.activation(halo[:, pr, j, :], p_ip[:, GT - 3:GT], ACT.Copy).then_inc(ip_free, 1)
                act.wait_ge(raw_done, n + 1)
                a_.activation(xs[:, pr, j, :], xraw[:, buf, 3:3 + GT], ACT.Identity, bias=cb_[:, j:j + 1],
                              scale=cw[:, j, 3:4]).then_inc(tap3_done, 1)

            def step(b, q, gn, ap, bk, tl):
                s = b * NQ + q
                g, h, t = s - 1, s - 2, s - 3
                pa, pb = (q - 1) % 2, q % 2
                last = isinstance(b, int) and b >= B - 1
                hi = gn and q == NQ - 1 and not last
                if gn and not ap:
                    lap_hi(*fill(b, q, 0))
                if gn and bk and not tl:
                    act.wait_ge(llo_dve, low_halves(len(l_items))[0])
                    act.wait_ge(llo_pool, low_halves(len(l_items))[1])
                if bk:
                    exps(h, 1, pb)
                elif ap:
                    lap_hi(*fill(b, q, 0))
                if ap:
                    act.wait_ge(t_mm, g + 1)
                    wait(act, ip_mm, 5 * g)
                    a_.activation(xnT[:, :], p_front[:, :], ACT.Copy).then_inc(xnT_done, 1)
                if bk:
                    exps(h, 2, pb)
                elif ap:
                    lap_hi(*fill(b, q, 1))
                if ap:
                    act.wait_ge(nab_done, g + 1)
                    a_.activation(e_dt[:, :], nab[:, :], ACT.Exp).then_inc(e_done, 1)
                    conv_in(g, 0, 2, pa, (q - 1) % 4 == 0)
                if hi:
                    act.wait_ge(gn_mm, 4 * s + 1)
                    split_hi(0, 4 * (b + 1) + 1)
                if ap and not bk:
                    lap_hi(*fill(b, q, 2))
                if ap:
                    conv_in(g, 1, 0, pa, (q - 1) % 4 == 0)
                if bk:
                    exps(h, 3, pb)
                elif ap:
                    lap_hi(*fill(b, q, 3))
                if ap:
                    act.wait_ge(cum_mm, g + 1)
                    a_.activation(cum[:, pa, :], p_front[:, 32:48], ACT.Copy).then_inc(cum_done, 1)
                    conv_in(g, 2, 1, pa, (q - 1) % 4 == 0)
                    act.wait_ge(parts_mm, g + 1)
                    a_.activation(cumT[:, pa, :], p_cumT, ACT.Copy).then_inc(cumT_done, 1)
                if hi:
                    act.wait_ge(gn_mm, 4 * s + 2)
                    split_hi(1, 4 * (b + 1) + 2)
                if ap:
                    for i, j in enumerate((2, 0, 1)):
                        act.wait_ge(conv_done, 3 * g + i + 1)
                        a_.activation(xs[:, pa, j, :], xs[:, pa, j, :], ACT.Silu).then_inc(silu_done, 1)
                    act.wait_ge(ip_mm, 5 * g + 4)
                    wait(act, gate_done, g - 1)
                    a_.activation(sz[:, pa, 0, :], p_ip[:, :], ACT.Silu).then_inc(silu_done, 1)
                if hi:
                    act.wait_ge(gn_mm, 4 * s + 3)
                    split_hi(2, 4 * (b + 1) + 3)
                if bk:
                    act.wait_ge(gate_done, h + 1)
                    wait(act, conv_done, 3 * (h + 2) if not isinstance(h, int) else 3 * min(h + 2, G_ALL))
                    a_.activation(ysq, xs[:, pb, 0:2, :], ACT.Square).then_inc(sq_done, 1)
                if ap:
                    act.wait_ge(ip_mm, 5 * g + 5)
                    a_.activation(sz[:, pa, 1, :], p_ip[:, :], ACT.Silu).then_inc(silu_done, 1)
                if gn:
                    act.wait_ge(gn_mm, 4 * s + 4)
                    wait(act, t_mm, s)
                    a_.activation(gT_xn[:, :], p_gn[:, :], ACT.Copy,
                                  scale=1.0 / (L_SCALE * X_SCALE)).then_inc(gT_done, 1)
                if gn and not ap:
                    lap_hi(*fill(b, q, 1))
                if hi:
                    split_hi(3, 4 * (b + 1) + 4)
                if ap:
                    exps(g, 0, pa)

            every_step(act, step)

        @block.vector
        def _(dve):
            v_ = nc.vector
            v_.memset(dce[:, :, :], 0.0)

            def stats1(n, q, nth, cs=range(GC)):
                wait(dve, mv1_done, n)
                dve.wait_ge(xh_in[q % 2], 16 * nth)
                for c in cs:
                    last = v_.bn_stats(st1[:, c, :], xhat[:, q * GC + c, :])
                if c == GC - 1:
                    last.then_inc(st1_done, 1)

            def aggr1(n):
                dve.wait_ge(st1_done, n + 1)
                wait_apart(dve, xh_done, n)
                for c in range(GC):
                    last = v_.bn_aggr(mv1[:, c, :], st1[:, c, :])
                last.then_inc(mv1_done, 1)

            def split_lo(kk, count):
                dve.wait_ge(hi_done, count)
                v_.scalar_tensor_tensor(lnx[:, 4 * kk:4 * kk + 4, 1, :], xhat[:, 4 * kk:4 * kk + 4, :], X_SCALE,
                                        lnx[:, 4 * kk:4 * kk + 4, 0, :], ALU.mult, ALU.subtract).then_inc(lo_done, 1)

            v_.memset(rsp[:, 0:KT:4, NQ:NQ + 1], 0.0).then_inc(relu_dve, 1)
            n_dve = 1
            for m, (kind, j, i0, n) in enumerate(bank_items):
                if kind == "sum":
                    dve.wait_ge(sym_mm, m + 1)
                    dst = S_[:, i0:i0 + n, j * P:(j + 1) * P]
                    v_.tensor_tensor(dst, dst, bank[m % 8][:, 0:n * P].rearrange("p (i n) -> p i n", i=n),
                                     ALU.add).then_inc(sym_add, 1)
                if m + 1 == strip_end(j):
                    if j == 4:
                        dve.wait_ge(aexp_done, 1)
                        v_.tensor_scalar(aneg[:, :], aexp[:, :], -1.0, None, ALU.mult).then_inc(aneg_done, 1)
                    if j in (4, 6, 8, 10):
                        nb = (j - 4) // 2
                        stats1(nb, nb, nb // 2 + 1)
                        aggr1(nb)
                    if j in (8, 10, 12, 14):
                        split_lo((j - 8) // 2, (j - 8) // 2 + 1)
                    if any(dve_upper(k, q) for k, q in uppers[j]):
                        dve.wait_ge(sym_mm, m + 1)
                        dve.wait_ge(sym_add, items_to("sum", m + 1))
                    for k, q in uppers[j]:
                        if dve_upper(k, q):
                            v_.scalar_tensor_tensor(upper_row(k, q), upper_row(k, q), 0.0, upper_row(k, q), ALU.max, ALU.max,
                                                    accum_out=rsp[:, k, q:q + 1]).then_inc(relu_dve, 1)
                            n_dve += 1
            dve.wait_ge(relu_act, n_relus - (n_dve - 1))
            dve.wait_ge(relu_dve, n_dve)
            v_.tensor_reduce(out=rsum[:, :], in_=rsp[:, :, :], axis=mybir.AxisListType.X,
                             op=ALU.add).then_inc(rsum_done, 1)
            dve.wait_ge(wc_mm, 1)
            for j in range(2):
                last = v_.tensor_scalar(wc[:, j, :], p_e[:, j * P:(j + 1) * P], nwc[:, j:j + 1], None, ALU.mult)
            last.then_inc(wc_done, 1)

            def diagonal(q):
                dve.wait_ge(cinv_done, 5)
                wait(dve, cbc_mm, q - 1)
                v_.tensor_tensor(diag[:, q % 2, :, :], over(ident[:, :], 1, GC), over(cinv[:, q * GC:(q + 1) * GC], 2, P),
                                 ALU.mult).then_inc(diag_done, 1)

            def lap_lo(m):
                if m >= 0 and not on_pool(m):
                    k, q = l_items[m]
                    dve.wait_ge(lhi_done, m + 1)
                    v_.tensor_tensor(L_[:, k, q, 1, :], ring[m % RING], L_[:, k, q, 0, :],
                                     ALU.subtract).then_inc(llo_dve, 1)

            def lap(m0, m1):
                for m in range(m0, m1):
                    k, q = l_items[m]
                    if m >= RING:
                        if on_pool(m - RING):
                            dve.wait_ge(llo_pool, low_halves(m - RING + 1)[1])
                        else:
                            dve.wait_ge(llo_dve, low_halves(m - RING + 1)[0])
                    if k == 0:
                        dve.wait_ge(cbc_mm, q + 1)
                    v_.scalar_tensor_tensor(ring[m % RING], S_[:, k, q * GT:(q + 1) * GT], negc[:, k:k + 1],
                                            p_col[q][:, :], ALU.mult, ALU.mult).then_inc(lt_done, 1)
                    if k // 4 == q:
                        dve.wait_ge(lt_done, m + 1)
                        dg = ring[m % RING][:, (k % 4) * P:(k % 4 + 1) * P]
                        v_.scalar_tensor_tensor(dg, ident[:, :], L_SCALE, dg, ALU.mult, ALU.add).then_inc(ld_done, 1)
                    if m - LAG not in drained:
                        lap_lo(m - LAG)

            drained = range(KT - LAG, KT)
            diagonal(0)
            diagonal(1)
            lap(0, 12)
            diagonal(2)
            lap(12, 14)
            diagonal(3)
            lap(14, KT)
            for m in drained:
                lap_lo(m)

            def keep_last(h, c):
                dve.wait_ge(l_exp, 4 * h + c + 1)
                wait(dve, xdd_done, 4 * h + c - 1)
                v_.tensor_copy(dcy[:, c % 2, :], Lx[:, c % 2, :, P - 1]).then_inc(dcy_done, 1)

            def operands(h, c, pr, first):
                cb = c % 2
                tg = p_tg[cb]
                if first and c == 0:
                    wait(dve, yst_done, 4 * h)
                    v_.memset(state[:, 0, :, :], 0.0)
                dve.wait_ge(g_mm, 4 * h + c + 1)
                wait(dve, m_done, 4 * h + c)
                v_.tensor_tensor(Gm[:, :], tg[:, 320:448], upper[:, :], ALU.mult).then_inc(gm_done, 1)
                wait(dve, mid_mm, 4 * h + c - 1)
                wait(dve, xdd_done, 4 * h + c - 1)
                v_.tensor_tensor(xdtp[:, cb, :, 0:HD], tg[:, 0:DI].rearrange("p (h d) -> p h d", h=H),
                                 over(dtv[:, pr, c * H:(c + 1) * H], 2, HD), ALU.mult).then_inc(xdt_done, 1)
                v_.tensor_copy(Bp[:, cb, DS:2 * DS], tg[:, DI:DI + DS])

            def decayed_g(h, c):
                cb = c % 2
                dve.wait_ge(dcy_done, 4 * h + c + 1)
                dve.wait_ge(gm_done, 4 * h + c + 1)
                v_.tensor_tensor(Lx[:, cb, :, :], over(Gm[:, :], 1, H), Lx[:, cb, :, :],
                                 ALU.mult).then_inc(m_done, 1)

            def pre(h, c, pr, first):
                keep_last(h, c)
                operands(h, c, pr, first)
                decayed_g(h, c)

            def post_state(h, c, js=range(2)):
                cb = c % 2
                dve.wait_ge(mid_mm, 4 * h + c + 1)
                for j in js:
                    for hh in range(2):
                        rows = slice(hh * DS, (hh + 1) * DS)
                        v_.scalar_tensor_tensor(
                            state[rows, 1 - cb, j, hh * HD:(hh + 1) * HD], state[rows, cb, j, hh * HD:(hh + 1) * HD],
                            dce[rows, cb, j:j + 1], p_y[rows, 2 * P + j * HD:2 * P + (j + 1) * HD], ALU.mult, ALU.add)

            def post_y(h, c, pr):
                for j in range(2):
                    xc = xs[:, pr, j, c * P:(c + 1) * P]
                    last = v_.scalar_tensor_tensor(xc, xc, dcol[:, j:j + 1], p_y[:, j * P:(j + 1) * P],
                                                   ALU.mult, ALU.add)
                last.then_inc(yst_done, 1)

            def link(g, n, pr):
                z, z2, poly = (ch[:, i, :] for i in range(3))
                if n == 0:
                    dve.wait_ge(e_done, g + 1)
                else:
                    wait_apart(dve, chain, DT_OPS * g + n)
                if n == 0:
                    ins = v_.tensor_scalar(z, e_dt[:, :], 2.0, None, ALU.add)
                elif n == 1:
                    ins = v_.reciprocal(z, z)
                elif n == 2:
                    ins = v_.tensor_tensor(z, e_dt[:, :], z, ALU.mult)
                elif n == 3:
                    ins = v_.tensor_tensor(z2, z, z, ALU.mult)
                elif n == 4:
                    ins = v_.tensor_scalar(poly, z2, ATANH[4], None, ALU.mult)
                elif n <= 7:
                    ins = v_.scalar_tensor_tensor(poly, poly, ATANH[8 - n], z2, ALU.add, ALU.mult)
                elif n == 8:
                    ins = v_.scalar_tensor_tensor(poly, poly, ATANH[0], z, ALU.add, ALU.mult)
                elif n == 9:
                    ins = v_.scalar_tensor_tensor(dtv[:, pr, :], v_dt[:, :], 0.0, poly, ALU.max, ALU.add)
                else:
                    ins = v_.tensor_tensor(dA[:, :].rearrange("p (c h) -> p c h", h=H),
                                           dtv[:, pr, :].rearrange("p (c h) -> p c h", h=H),
                                           over(aneg[:, :], 1, GC), ALU.mult)
                ins.then_inc(chain if n < DT_OPS else dA_done, 1)

            def conv_tap(g, i, j, k, pr):
                buf = (pr + i) % 2
                if k == 2:
                    dve.wait_ge(tap3_done, 3 * g + i + 1)
                else:
                    dve.wait_ge(tap, 6 * g + 2 * i + 2 - k)
                acc = xs[:, pr, j, :]
                v_.scalar_tensor_tensor(acc, xraw[:, buf, k:k + GT], cw[:, j, k:k + 1], acc,
                                        ALU.mult, ALU.add).then_inc(tap if k else conv_done, 1)

            def step(b, q, gn, ap, bk, tl):
                s = b * NQ + q
                g, h, t = s - 1, s - 2, s - 3
                qa, qt = (q - 1) % 4, (q - 3) % 4
                pa, pb = (q - 1) % 2, q % 2
                first = (q - 2) % 4 == 0
                last = isinstance(b, int) and b >= B - 1
                ln1 = gn and not last
                nth = 2 * (b + 1) + q // 2 + 1
                if gn and not ap:
                    lap(*fill(b, q, 0))
                    lap(*fill(b, q, 1))
                if ap:
                    dve.wait_ge(w_mm, g + 1)
                    dve.wait_ge(x_in[pa], 16 * of_parity(b, q, 1))
                    xt = x1[:, qa, :, :]
                    v_.scalar_tensor_tensor(xt, p_front[:, :].rearrange("p (c f) -> p c f", c=GC), 0.0, xt,
                                            ALU.max, ALU.add).then_inc(x1_done, 1)
                if ap:
                    dve.wait_ge(x1_done, g + 1)
                    for c in range(GC):
                        ins = v_.bn_stats(st2[:, c, :], x1[:, qa, c, :])
                    ins.then_inc(st2_done, 1)
                if tl:
                    dve.wait_ge(ss_mm, t + 1)
                    wait(dve, rms_done, t)
                    v_.tensor_scalar(ssm[:, :], p_y[:, 384:384 + GC], EPS, None, ALU.add).then_inc(ss_done, 1)
                if ap:
                    wait_apart(dve, st2_done, g + 1)
                    for c in range(GC):
                        ins = v_.bn_aggr(mv2[:, c, :], st2[:, c, :])
                    ins.then_inc(mv2_done, 1)
                if bk:
                    pre(h, 0, pb, first)
                elif ap:
                    lap(*fill(b, q, 0))
                if ap:
                    dve.wait_ge(rs2_done, g + 1)
                    for c in range(GC):
                        ins = v_.tensor_scalar(gT_xn[:, c * P:(c + 1) * P], x1[:, qa, c, :], mv2[:, c, 0:1],
                                               rs2[:, c:c + 1], ALU.subtract, ALU.mult)
                    ins.then_inc(xn_done, 1)
                if tl:
                    dve.wait_ge(out_mm, t + 1)
                    dve.wait_ge(rms_done, t + 1)
                    dve.wait_ge(xb_done, t + 1)
                    for c in range(GC):
                        xt = x1[:, qt, c, :]
                        ins = v_.scalar_tensor_tensor(xt, p_ip[:, c * P:(c + 1) * P], rms[:, c:c + 1], xt,
                                                      ALU.mult, ALU.add)
                    ins.then_inc(out_done, 1)
                if bk:
                    pre(h, 1, pb, first)
                    post_state(h, 0)
                    post_y(h, 0, pb)
                elif ap:
                    lap(*fill(b, q, 1))
                if bk:
                    operands(h, 2, pb, first)
                if ap:
                    dve.wait_ge(dt_mm, g + 1)
                    wait(dve, dA_done, g)
                    v_.tensor_tensor(v_dt[:, :].rearrange("p (c h) -> p c h", h=H),
                                     p_front[:, 0:16].rearrange("p (c h) -> p c h", h=H),
                                     over(dtb[:, :], 1, GC), ALU.add).then_inc(v_done, 1)
                if bk:
                    keep_last(h, 2)
                if ln1:
                    stats1(s + NQ, q, nth, [0])
                if ap:
                    dve.wait_ge(v_done, g + 1)
                    v_.scalar_tensor_tensor(nab[:, :], v_dt[:, :], -1.0, v_dt[:, :], ALU.mult, ALU.min).then_inc(nab_done, 1)
                if bk:
                    decayed_g(h, 2)
                elif ap:
                    lap(*fill(b, q, 2))
                if ap:
                    link(g, 0, pa)
                if ln1:
                    stats1(s + NQ, q, nth, [1])
                if ap:
                    link(g, 1, pa)
                if ln1:
                    stats1(s + NQ, q, nth, [2])
                if ap:
                    link(g, 2, pa)
                if ln1:
                    stats1(s + NQ, q, nth, [3])
                if ap:
                    link(g, 3, pa)
                if bk:
                    post_state(h, 1, [0])
                if ap:
                    link(g, 4, pa)
                if bk:
                    post_state(h, 1, [1])
                if ap:
                    link(g, 5, pa)
                if bk:
                    post_y(h, 1, pb)
                if ap:
                    link(g, 6, pa)
                if ln1:
                    aggr1(s + NQ)
                if ap:
                    link(g, 7, pa)
                    conv_tap(g, 0, 2, 2, pa)
                    link(g, 8, pa)
                    conv_tap(g, 0, 2, 1, pa)
                    link(g, 9, pa)
                    conv_tap(g, 0, 2, 0, pa)
                    link(g, 10, pa)
                    conv_tap(g, 1, 0, 2, pa)
                if bk:
                    pre(h, 3, pb, first)
                elif ap:
                    lap(*fill(b, q, 3))
                    for m in range(len(l_items) - LAG, len(l_items)):
                        lap_lo(m)
                if ap:
                    conv_tap(g, 1, 0, 1, pa)
                if bk:
                    post_state(h, 2)
                    post_y(h, 2, pb)
                if ap:
                    conv_tap(g, 1, 0, 0, pa)
                if ap:
                    for k in (2, 1, 0):
                        conv_tap(g, 2, 1, k, pa)
                if bk:
                    post_state(h, 3)
                    post_y(h, 3, pb)
                    dve.wait_ge(silu_done, 5 * h + 5)
                    dve.wait_ge(yst_done, 4 * h + 4)
                    v_.tensor_tensor(xs[:, pb, 0:2, :], xs[:, pb, 0:2, :], sz[:, pb, :, :],
                                     ALU.mult).then_inc(gate_done, 1)
                if ln1 and q == NQ - 1:
                    for kk in range(4):
                        split_lo(kk, 4 * (b + 1) + kk + 1)

            every_step(dve, step)

        @block.tensor
        def _(pe):
            t_ = nc.tensor
            pe.wait_ge(consts_pool, 1)
            for m, (kind, j, i0, n) in enumerate(bank_items):
                if m == 0 or bank_items[m - 1][1] != j:
                    pe.wait_ge(adj_in[j], 16)
                if m >= 8:
                    if bank_items[m - 8][0] == "sum":
                        pe.wait_ge(sym_add, items_to("sum", m - 7))
                    else:
                        pe.wait_ge(relu_act, relus_before(m - 8) + 1)
                if kind == "mirror":
                    pe.wait_ge(sym_add, 1 + sum_index(j, i0))
                for i in range(n):
                    src = S_[:, j, (i0 + i) * P:(i0 + i + 1) * P] if kind == "sum" \
                        else S_[:, i0 + i, j * P:(j + 1) * P]
                    last = t_.transpose(bank[m % 8][:, i * P:(i + 1) * P], src, ident[:, :])
                last.then_inc(sym_mm, 1)
            pe.wait_ge(relu_act, relus_before(len(bank_items)))
            pe.wait_ge(sym_add, n_sums)
            pe.wait_ge(w_landed, 16 * 12)
            for j in range(2):
                last = t_.transpose(p_front[:, j * P:(j + 1) * P], wo[:, j, :], ident[:, :])
            last.then_inc(wot_mm, 1)
            pe.wait_ge(wot_done, 1)
            for j in range(2):
                last = t_.matmul(p_e[:, j * P:(j + 1) * P], woT[:, j, :], wl, start=True, stop=True)
            last.then_inc(wc_mm, 1)
            pe.wait_ge(wc_done, 1)
            for q in range(NQ):
                pe.wait_ge(diag_done, q + 1)
                t_.matmul(p_col[q][:, :], ones, diag[:, q % 2, :, :].rearrange("p t n -> p (t n)"), start=True,
                          stop=True).then_inc(cbc_mm, 1)

            def laplacian(b, q, m0, m1):
                s = b * NQ + q
                for m in range(m0, m1):
                    k, term = m // 3, m % 3
                    if m == 0:
                        wait(pe, gT_done, s)
                        if isinstance(b, int) and b == 0:
                            pe.wait_ge(llo_dve, low_halves(KT * (q + 1))[0])
                            pe.wait_ge(llo_pool, low_halves(KT * (q + 1))[1])
                    if q == 0 and m % 12 == 0:
                        pe.wait_ge(lo_done, 4 * b + m // 12 + 1)
                        pe.wait_ge(hi_done, 4 * b + m // 12 + 1)
                    ins = t_.matmul(p_gn[:, :], lnx[:, k, term // 2, :], L_[:, k, q, term % 2, :],
                                    start=(m == 0), stop=(m == 3 * KT - 1))
                    if m % 12 == 11:
                        ins.then_inc(gn_mm, 1)

            def chunk_in(h, c, pr):
                cb = c % 2
                tg = p_tg[cb]
                cs = slice(c * P, (c + 1) * P)
                rows = cumT[:, pr, :]
                pe.wait_ge(cumT_done, h + 1)
                wait(pe, e_exp, 4 * h + c)
                for j in range(2):
                    ins = t_.matmul(p_e[:, j * P:(j + 1) * P], pick[:, c * H + 2 * j:c * H + 2 * j + 2, :].rearrange("r h d -> r (h d)"),
                                    rows, start=True, stop=True)
                ins.then_inc(e_mm, 1)
                wait(pe, drop_done, 4 * h + c)
                for hh in range(H):
                    ins = t_.matmul(p_diff[:, hh * P:(hh + 1) * P], over(pick[:, c * H + hh, 0], 1, P), rows,
                                    start=True, stop=True)
                ins.then_inc(diff_mm, 1)
                if c == 0:
                    pe.wait_ge(silu_done, 5 * h + 3)
                    pe.wait_ge(cc_in, 32 * h + 32)
                wait(pe, m_done, 4 * h + c - 1)
                t_.transpose(tg[:, 0:P], xs[:, pr, 0, cs], ident[:, :])
                t_.transpose(tg[:, P:2 * P], xs[:, pr, 1, cs], ident[:, :])
                t_.transpose(tg[:, DI:DI + DS], xs[0:DS, pr, 2, cs], ident[0:DS, 0:DS])
                t_.matmul(tg[:, 320:448], xs[0:DS, pr, 2, cs], CC[0:DS, cs], start=True, stop=True).then_inc(g_mm, 1)

            def chunk_out(h, c, tl):
                cb = c % 2
                pe.wait_ge(m_done, 4 * h + c + 1)
                pe.wait_ge(ce_done, 4 * h + c + 1)
                wait(pe, yst_done, 4 * h + c)
                if c == 0 and tl:
                    pe.wait_ge(ss_done, h)
                for j in range(2):
                    y = p_y[:, j * P:(j + 1) * P]
                    xp = xdtb[:, cb, :]
                    t_.matmul(y, xp[:, 4 * j * HD:4 * j * HD + P], Lx[:, cb, 2 * j, :], start=True, stop=False)
                    t_.matmul(y, xp[:, (4 * j + 1) * HD:(4 * j + 1) * HD + P], Lx[:, cb, 2 * j + 1, :],
                              start=False, stop=False)
                    t_.matmul(y, state[:, cb, j, :], CE[:, cb, j, :], start=False, stop=True)
                pe.wait_ge(xdd_done, 4 * h + c + 1)
                for hh in range(2):
                    ins = t_.matmul(p_y[:, 2 * P:3 * P], Bp[:, cb, (1 - hh) * DS:(1 - hh) * DS + P],
                                    xdd[:, cb, hh, :, :].rearrange("p j d -> p (j d)"), start=(hh == 0), stop=(hh == 1))
                ins.then_inc(mid_mm, 1)

            def project(g, i):
                col = (DI + 2 * P, DI, DI + P, 0, P)[i]
                if i in (1, 2, 3):
                    pe.wait_ge(ip_free, 3 * g + i)
                else:
                    wait(pe, silu_done, 5 * g + i)
                if i == 0:
                    wait(pe, out_done, g - 1)
                t_.matmul(p_ip[:, :], w_in[:, col:col + P], xnT[:, :], start=True, stop=True).then_inc(ip_mm, 1)

            def step(b, q, gn, ap, bk, tl):
                s = b * NQ + q
                g, h, t = s - 1, s - 2, s - 3
                pa, pb, pt = (q - 1) % 2, q % 2, (q - 3) % 2
                if ap:
                    pe.wait_ge(gT_done, g + 1)
                    wait(pe, cumT_done, g)
                    for c in range(GC):
                        ins = t_.matmul(p_front[:, c * P:(c + 1) * P], gT_xn[:, c * P:(c + 1) * P], w_gnn[:, :],
                                        start=True, stop=True)
                    ins.then_inc(w_mm, 1)
                if gn:
                    laplacian(b, q, 0, 6)
                if tl:
                    pe.wait_ge(sqs_done, t + 1)
                    pe.wait_ge(yst_done, 4 * t + 4)
                    for c in range(GC):
                        ins = t_.matmul(p_y[:, 384 + c:385 + c], ysq[:, 0, c * P:(c + 1) * P], onec[:, :],
                                        start=True, stop=True)
                    ins.then_inc(ss_mm, 1)
                    wait(pe, silu_done, 5 * (t + 2) if not isinstance(t, int) else 5 * min(t + 2, G_ALL))
                    for c in range(GC):
                        for j in range(2):
                            ins = t_.matmul(p_ip[:, c * P:(c + 1) * P], xs[:, pt, j, c * P:(c + 1) * P], wc[:, j, :],
                                            start=(j == 0), stop=(j == 1))
                    ins.then_inc(out_mm, 1)
                if bk:
                    chunk_in(h, 1, pb)
                    chunk_out(h, 0, tl)
                if gn:
                    laplacian(b, q, 6, 12)
                if ap:
                    pe.wait_ge(xn_done, g + 1)
                    for c in range(GC):
                        ins = t_.transpose(p_front[:, c * P:(c + 1) * P], gT_xn[:, c * P:(c + 1) * P], ident[:, :])
                    ins.then_inc(t_mm, 1)
                if bk:
                    chunk_in(h, 2, pb)
                if gn:
                    laplacian(b, q, 12, 13)
                if ap:
                    pe.wait_ge(xnT_done, g + 1)
                    for c in range(GC):
                        ins = t_.matmul(p_front[:, c * H:(c + 1) * H], xnT[:, c * P:(c + 1) * P],
                                        w_in[:, 2 * DI + 2 * DS:2 * DI + 2 * DS + H], start=True, stop=True)
                    ins.then_inc(dt_mm, 1)
                    project(g, 0)
                if bk:
                    chunk_out(h, 1, tl)
                if ap:
                    project(g, 1)
                if bk:
                    chunk_in(h, 3, pb)
                if gn:
                    laplacian(b, q, 13, 27)
                if ap:
                    pe.wait_ge(dA_done, g + 1)
                    t_.matmul(p_front[:, 32:48], upper[:, :], dA[:, :], start=True, stop=True).then_inc(cum_mm, 1)
                if bk:
                    chunk_out(h, 2, tl)
                if ap:
                    project(g, 2)
                if gn:
                    laplacian(b, q, 27, 34)
                if ap:
                    wait_apart(pe, parts_done, g + 1)
                    t_.transpose(p_cumT, parts[:, :, :].rearrange("p a b -> p (a b)"), identb[:, :]).then_inc(parts_mm, 1)
                if bk:
                    chunk_out(h, 3, tl)
                if ap:
                    project(g, 3)
                if gn:
                    laplacian(b, q, 34, 42)
                if ap:
                    project(g, 4)
                if gn:
                    laplacian(b, q, 42, 48)
                if ap and not bk:
                    pe.wait_ge(lt_done, len(l_items))
                if ap:
                    chunk_in(g, 0, pa)

            every_step(pe, step)


_INS = ["x", "adj", "L0_gnn_W", "L0_ffn_W_in", "L0_ffn_conv_w", "L0_ffn_conv_b", "L0_ffn_dt_bias", "L0_ffn_A_log",
        "L0_ffn_D", "L0_ffn_norm_w", "L0_ffn_W_out", "L0_ffn_W_lin", "L0_ffn_b_lin"]


def kernel(**inputs):
    import numpy as _np
    import concourse.bacc as _bacc
    from concourse import mybir as _mybir
    from concourse.bass_utils import run_bass_kernel_spmd as _run

    nc = _bacc.Bacc("TRN2", target_bir_lowering=False, num_devices=1)
    arrays, args = {}, []
    for name in _INS:
        a = _np.ascontiguousarray(inputs[name])
        arrays[f"in_{name}"] = a
        args.append(nc.dram_tensor(f"in_{name}", a.shape, _mybir.dt.from_np(a.dtype), kind="ExternalInput").ap())
    o = nc.dram_tensor("out", (B, N, F), F32, kind="ExternalOutput").ap()
    gnn_mamba(nc, *args, o)
    r = _run(nc, [arrays], core_ids=[0])
    return r.results[0]["out"]
```
